# Optimizing a Trainium2 kernel written in Bass

```python
import numpy as np
import jax
import jax.numpy as jnp

def _softmax(x, axis=-1):
    return jax.nn.softmax(x, axis=axis)

def _gelu(x):
    return jax.nn.gelu(x, approximate=True)

def _silu(x):
    return jax.nn.silu(x)

def _sigmoid(x):
    return jax.nn.sigmoid(x)

def _layernorm(x, axis=-1, eps=1e-05):
    m = jnp.mean(x, axis=axis, keepdims=True)
    v = jnp.var(x, axis=axis, keepdims=True)
    return (x - m) / jnp.sqrt(v + eps)

def _scatter_add(tgt, idx, src, axis=0):
    return tgt.at[idx].add(src)

def _segment_sum(src, seg, n):
    return jax.ops.segment_sum(src, seg, n)
kernel_name = 'mk_xattn_seq_d2_seqx_r4_f3f353'

def setup_inputs(seed: int=0):
    np.random.seed(seed)
    _w = jnp.asarray

    def _rec_inputs():
        import jax
        import jax.numpy as jnp
        _rk = jax.random.key(seed)
        x = -0.000125 + 0.9999 * jax.random.normal(jax.random.fold_in(_rk, 1), (8, 100, 512), jnp.float32)
        _lenS = 100 - jax.random.randint(jax.random.fold_in(_rk, 7), (8,), 0, max(1, 100 // 4) + 1, jnp.int32)
        _lenS2 = 361 - jax.random.randint(jax.random.fold_in(_rk, 8), (8,), 0, max(1, 361 // 4) + 1, jnp.int32)
        _ctx_2048P = jax.random.normal(jax.random.fold_in(_rk, 11), (8, 16, 512), jnp.float32)
        _ctx_2048c = jax.random.dirichlet(jax.random.fold_in(_rk, 511), 0.3 * jnp.ones((16,), jnp.float32), (8, 361))
        _ctx_2048t = jnp.einsum('bsk,bkd->bsd', _ctx_2048c, _ctx_2048P)
        _ctx_2048t = _ctx_2048t * jax.lax.rsqrt(jnp.mean(jnp.square(_ctx_2048t)) + 1e-12) * 0.953939
        ctx_2048 = -0.00401388 + 1.00018 * (_ctx_2048t + 0.3 * jax.random.normal(jax.random.fold_in(_rk, 611), (8, 361, 512), jnp.float32))
        return (x, ctx_2048)
    x, ctx_2048 = _rec_inputs()

    def _L0_xattn_setup():
        import jax, jax.numpy as jnp
        import numpy as np
        H = 512
        B, L, S = (4, 1024, 10)
        key = jax.random.key(seed)
        k1, k2, k3, k4, k5, k6 = jax.random.split(key, 6)
        scale = 1.0 / np.sqrt(H)
        return {'h_english': jax.random.normal(k1, (B, L, H), dtype=jnp.float32), 'h_lojban': jax.random.normal(k2, (B, S, H), dtype=jnp.float32), 'w_q': jax.random.normal(k3, (H, H), dtype=jnp.float32) * scale, 'w_k': jax.random.normal(k4, (H, H), dtype=jnp.float32) * scale, 'w_v': jax.random.normal(k5, (H, H), dtype=jnp.float32) * scale, 'w_o': jax.random.normal(k6, (H, H), dtype=jnp.float32) * scale, 'alpha': jnp.float32(0.1)}
    _L0_xattn_all = _L0_xattn_setup()
    _L0_xattn_in = {k: v for k, v in _L0_xattn_all.items() if k in ('w_q', 'w_k', 'w_v', 'w_o', 'alpha')}
    del _L0_xattn_all

    def _L1_xattn_setup():
        import jax, jax.numpy as jnp
        import numpy as np
        B, Q, S1, S2 = (4, 64, 512, 512)
        D, H, K, F = (512, 16, 128, 2048)
        LN_EPS = 1e-05

        def _layer_norm(x, scale, offset):
            mu = jnp.mean(x, axis=-1, keepdims=True)
            var = jnp.var(x, axis=-1, keepdims=True)
            return (x - mu) * jax.lax.rsqrt(var + LN_EPS) * scale + offset

        def _cross_attention(q_in, kv_in, wq, bq, wk, bk, wv, bv, wo, bo, bias_k, bias_v):
            b, q_len, _ = q_in.shape
            t = kv_in.shape[1]
            qh = (q_in @ wq + bq).reshape(b, q_len, H, K)
            kh = (kv_in @ wk + bk).reshape(b, t, H, K)
            vh = (kv_in @ wv + bv).reshape(b, t, H, K)
            kh = jnp.concatenate([kh, jnp.broadcast_to(bias_k, (b, 1, H, K))], axis=1)
            vh = jnp.concatenate([vh, jnp.broadcast_to(bias_v, (b, 1, H, K))], axis=1)
            scale = jnp.sqrt(jnp.asarray(K, q_in.dtype))
            logits = jnp.einsum('bqhk,bthk->bhqt', qh, kh) / scale
            weights = jax.nn.softmax(logits, axis=-1)
            ctx = jnp.einsum('bhqt,bthk->bqhk', weights, vh).reshape(b, q_len, H * K)
            return ctx @ wo + bo

        def _forward(x, xf_1, xf_2, ln1_scale, ln1_offset, wq1, bq1, wk1, bk1, wv1, bv1, wo1, bo1, bias_k1, bias_v1, ln2_scale, ln2_offset, wq2, bq2, wk2, bk2, wv2, bv2, wo2, bo2, bias_k2, bias_v2, ln_mlp_scale, ln_mlp_offset, w_fc1, b_fc1, w_fc2, b_fc2):
            res = x
            h = _layer_norm(x, ln1_scale, ln1_offset)
            x = res + _cross_attention(h, xf_1, wq1, bq1, wk1, bk1, wv1, bv1, wo1, bo1, bias_k1, bias_v1)
            res = x
            h = _layer_norm(x, ln2_scale, ln2_offset)
            x = res + _cross_attention(h, xf_2, wq2, bq2, wk2, bk2, wv2, bv2, wo2, bo2, bias_k2, bias_v2)
            h = _layer_norm(x, ln_mlp_scale, ln_mlp_offset)
            h = jax.nn.gelu(h @ w_fc1 + b_fc1, approximate=False) @ w_fc2 + b_fc2
            return x + h
        key = jax.random.key(seed)
        ks = iter(jax.random.split(key, 64))

        def rn(shape, s=0.02):
            return jax.random.normal(next(ks), shape, jnp.float32) * s
        inp = {'x': rn((B, Q, D), 1.0), 'xf_1': rn((B, S1, D), 1.0), 'xf_2': rn((B, S2, D), 1.0)}
        for i in (1, 2):
            inp[f'ln{i}_scale'] = jnp.ones((D,), jnp.float32)
            inp[f'ln{i}_offset'] = jnp.zeros((D,), jnp.float32)
            inp[f'wq{i}'] = rn((D, H * K))
            inp[f'bq{i}'] = jnp.zeros((H * K,), jnp.float32)
            inp[f'wk{i}'] = rn((D, H * K))
            inp[f'bk{i}'] = jnp.zeros((H * K,), jnp.float32)
            inp[f'wv{i}'] = rn((D, H * K))
            inp[f'bv{i}'] = jnp.zeros((H * K,), jnp.float32)
            inp[f'wo{i}'] = rn((H * K, D))
            inp[f'bo{i}'] = jnp.zeros((D,), jnp.float32)
            inp[f'bias_k{i}'] = rn((1, 1, H, K))
            inp[f'bias_v{i}'] = rn((1, 1, H, K))
        inp['ln_mlp_scale'] = jnp.ones((D,), jnp.float32)
        inp['ln_mlp_offset'] = jnp.zeros((D,), jnp.float32)
        inp['w_fc1'] = rn((D, F))
        inp['b_fc1'] = jnp.zeros((F,), jnp.float32)
        inp['w_fc2'] = rn((F, D))
        inp['b_fc2'] = jnp.zeros((D,), jnp.float32)
        return inp
    _L1_xattn_all = _L1_xattn_setup()
    _L1_xattn_in = {k: v for k, v in _L1_xattn_all.items() if k in ('ln1_scale', 'ln1_offset', 'wq1', 'bq1', 'wk1', 'bk1', 'wv1', 'bv1', 'wo1', 'bo1', 'bias_k1', 'bias_v1', 'ln2_scale', 'ln2_offset', 'wq2', 'bq2', 'wk2', 'bk2', 'wv2', 'bv2', 'wo2', 'bo2', 'bias_k2', 'bias_v2', 'ln_mlp_scale', 'ln_mlp_offset', 'w_fc1', 'b_fc1', 'w_fc2', 'b_fc2')}
    del _L1_xattn_all
    return {'x': x, 'ctx_2048': ctx_2048, 'L0_xattn_w_q': _L0_xattn_in['w_q'], 'L0_xattn_w_k': _L0_xattn_in['w_k'], 'L0_xattn_w_v': _L0_xattn_in['w_v'], 'L0_xattn_w_o': _L0_xattn_in['w_o'], 'L0_xattn_alpha': _L0_xattn_in['alpha'], 'L1_xattn_ln1_scale': _L1_xattn_in['ln1_scale'], 'L1_xattn_ln1_offset': _L1_xattn_in['ln1_offset'], 'L1_xattn_wq1': _L1_xattn_in['wq1'], 'L1_xattn_bq1': _L1_xattn_in['bq1'], 'L1_xattn_wk1': _L1_xattn_in['wk1'], 'L1_xattn_bk1': _L1_xattn_in['bk1'], 'L1_xattn_wv1': _L1_xattn_in['wv1'], 'L1_xattn_bv1': _L1_xattn_in['bv1'], 'L1_xattn_wo1': _L1_xattn_in['wo1'], 'L1_xattn_bo1': _L1_xattn_in['bo1'], 'L1_xattn_bias_k1': _L1_xattn_in['bias_k1'], 'L1_xattn_bias_v1': _L1_xattn_in['bias_v1'], 'L1_xattn_ln2_scale': _L1_xattn_in['ln2_scale'], 'L1_xattn_ln2_offset': _L1_xattn_in['ln2_offset'], 'L1_xattn_wq2': _L1_xattn_in['wq2'], 'L1_xattn_bq2': _L1_xattn_in['bq2'], 'L1_xattn_wk2': _L1_xattn_in['wk2'], 'L1_xattn_bk2': _L1_xattn_in['bk2'], 'L1_xattn_wv2': _L1_xattn_in['wv2'], 'L1_xattn_bv2': _L1_xattn_in['bv2'], 'L1_xattn_wo2': _L1_xattn_in['wo2'], 'L1_xattn_bo2': _L1_xattn_in['bo2'], 'L1_xattn_bias_k2': _L1_xattn_in['bias_k2'], 'L1_xattn_bias_v2': _L1_xattn_in['bias_v2'], 'L1_xattn_ln_mlp_scale': _L1_xattn_in['ln_mlp_scale'], 'L1_xattn_ln_mlp_offset': _L1_xattn_in['ln_mlp_offset'], 'L1_xattn_w_fc1': _L1_xattn_in['w_fc1'], 'L1_xattn_b_fc1': _L1_xattn_in['b_fc1'], 'L1_xattn_w_fc2': _L1_xattn_in['w_fc2'], 'L1_xattn_b_fc2': _L1_xattn_in['b_fc2']}

def reference(x, ctx_2048, L0_xattn_w_q, L0_xattn_w_k, L0_xattn_w_v, L0_xattn_w_o, L0_xattn_alpha, L1_xattn_ln1_scale, L1_xattn_ln1_offset, L1_xattn_wq1, L1_xattn_bq1, L1_xattn_wk1, L1_xattn_bk1, L1_xattn_wv1, L1_xattn_bv1, L1_xattn_wo1, L1_xattn_bo1, L1_xattn_bias_k1, L1_xattn_bias_v1, L1_xattn_ln2_scale, L1_xattn_ln2_offset, L1_xattn_wq2, L1_xattn_bq2, L1_xattn_wk2, L1_xattn_bk2, L1_xattn_wv2, L1_xattn_bv2, L1_xattn_wo2, L1_xattn_bo2, L1_xattn_bias_k2, L1_xattn_bias_v2, L1_xattn_ln_mlp_scale, L1_xattn_ln_mlp_offset, L1_xattn_w_fc1, L1_xattn_b_fc1, L1_xattn_w_fc2, L1_xattn_b_fc2):
    import jax
    import jax.numpy as jnp

    def _L0_xattn_ref(h_english, h_lojban, w_q, w_k, w_v, w_o, alpha):
        import jax, jax.numpy as jnp
        import numpy as np
        H = 512
        B, L, S = (4, 1024, 10)
        h = h_english.shape[-1]
        q = jnp.einsum('blh,oh->blo', h_english, w_q)
        k = jnp.einsum('bsh,oh->bso', h_lojban, w_k)
        v = jnp.einsum('bsh,oh->bso', h_lojban, w_v)
        scores = jnp.einsum('blh,bsh->bls', q, k) / jnp.sqrt(jnp.float32(h))
        probs = jax.nn.softmax(scores, axis=-1)
        context = jnp.einsum('bls,bsh->blh', probs, v)
        delta = jnp.einsum('blh,oh->blo', context, w_o)
        return h_english + alpha * delta

    def _L1_xattn_ref(x, xf_1, xf_2, ln1_scale, ln1_offset, wq1, bq1, wk1, bk1, wv1, bv1, wo1, bo1, bias_k1, bias_v1, ln2_scale, ln2_offset, wq2, bq2, wk2, bk2, wv2, bv2, wo2, bo2, bias_k2, bias_v2, ln_mlp_scale, ln_mlp_offset, w_fc1, b_fc1, w_fc2, b_fc2):
        import jax, jax.numpy as jnp
        import numpy as np
        B, Q, S1, S2 = (4, 64, 512, 512)
        D, H, K, F = (512, 16, 128, 2048)
        LN_EPS = 1e-05

        def _layer_norm(x, scale, offset):
            mu = jnp.mean(x, axis=-1, keepdims=True)
            var = jnp.var(x, axis=-1, keepdims=True)
            return (x - mu) * jax.lax.rsqrt(var + LN_EPS) * scale + offset

        def _cross_attention(q_in, kv_in, wq, bq, wk, bk, wv, bv, wo, bo, bias_k, bias_v):
            b, q_len, _ = q_in.shape
            t = kv_in.shape[1]
            qh = (q_in @ wq + bq).reshape(b, q_len, H, K)
            kh = (kv_in @ wk + bk).reshape(b, t, H, K)
            vh = (kv_in @ wv + bv).reshape(b, t, H, K)
            kh = jnp.concatenate([kh, jnp.broadcast_to(bias_k, (b, 1, H, K))], axis=1)
            vh = jnp.concatenate([vh, jnp.broadcast_to(bias_v, (b, 1, H, K))], axis=1)
            scale = jnp.sqrt(jnp.asarray(K, q_in.dtype))
            logits = jnp.einsum('bqhk,bthk->bhqt', qh, kh) / scale
            weights = jax.nn.softmax(logits, axis=-1)
            ctx = jnp.einsum('bhqt,bthk->bqhk', weights, vh).reshape(b, q_len, H * K)
            return ctx @ wo + bo

        def _forward(x, xf_1, xf_2, ln1_scale, ln1_offset, wq1, bq1, wk1, bk1, wv1, bv1, wo1, bo1, bias_k1, bias_v1, ln2_scale, ln2_offset, wq2, bq2, wk2, bk2, wv2, bv2, wo2, bo2, bias_k2, bias_v2, ln_mlp_scale, ln_mlp_offset, w_fc1, b_fc1, w_fc2, b_fc2):
            res = x
            h = _layer_norm(x, ln1_scale, ln1_offset)
            x = res + _cross_attention(h, xf_1, wq1, bq1, wk1, bk1, wv1, bv1, wo1, bo1, bias_k1, bias_v1)
            res = x
            h = _layer_norm(x, ln2_scale, ln2_offset)
            x = res + _cross_attention(h, xf_2, wq2, bq2, wk2, bk2, wv2, bv2, wo2, bo2, bias_k2, bias_v2)
            h = _layer_norm(x, ln_mlp_scale, ln_mlp_offset)
            h = jax.nn.gelu(h @ w_fc1 + b_fc1, approximate=False) @ w_fc2 + b_fc2
            return x + h
        return _forward(x, xf_1, xf_2, ln1_scale, ln1_offset, wq1, bq1, wk1, bk1, wv1, bv1, wo1, bo1, bias_k1, bias_v1, ln2_scale, ln2_offset, wq2, bq2, wk2, bk2, wv2, bv2, wo2, bo2, bias_k2, bias_v2, ln_mlp_scale, ln_mlp_offset, w_fc1, b_fc1, w_fc2, b_fc2)
    x = _L0_xattn_ref(x, ctx_2048, L0_xattn_w_q, L0_xattn_w_k, L0_xattn_w_v, L0_xattn_w_o, L0_xattn_alpha)
    x = _L1_xattn_ref(x, ctx_2048, ctx_2048, L1_xattn_ln1_scale, L1_xattn_ln1_offset, L1_xattn_wq1, L1_xattn_bq1, L1_xattn_wk1, L1_xattn_bk1, L1_xattn_wv1, L1_xattn_bv1, L1_xattn_wo1, L1_xattn_bo1, L1_xattn_bias_k1, L1_xattn_bias_v1, L1_xattn_ln2_scale, L1_xattn_ln2_offset, L1_xattn_wq2, L1_xattn_bq2, L1_xattn_wk2, L1_xattn_bk2, L1_xattn_wv2, L1_xattn_bv2, L1_xattn_wo2, L1_xattn_bo2, L1_xattn_bias_k2, L1_xattn_bias_v2, L1_xattn_ln_mlp_scale, L1_xattn_ln_mlp_offset, L1_xattn_w_fc1, L1_xattn_b_fc1, L1_xattn_w_fc2, L1_xattn_b_fc2)
    return x

_drawn_inputs = setup_inputs


def setup_inputs(seed=0):
    import zlib

    import numpy as np

    out = dict(_drawn_inputs(seed))
    spreads = {'L1_xattn_ln1_scale': (1.0, 0.6),
     'L1_xattn_ln1_offset': (0.0, 0.8),
     'L1_xattn_bq1': (0.0, 0.8),
     'L1_xattn_bk1': (0.0, 2.0),
     'L1_xattn_bv1': (0.0, 0.1),
     'L1_xattn_bo1': (0.0, 0.1),
     'L1_xattn_ln2_scale': (1.0, 0.6),
     'L1_xattn_ln2_offset': (0.0, 0.8),
     'L1_xattn_bq2': (0.0, 0.8),
     'L1_xattn_bk2': (0.0, 2.0),
     'L1_xattn_bv2': (0.0, 0.1),
     'L1_xattn_bo2': (0.0, 0.1),
     'L1_xattn_ln_mlp_scale': (1.0, 0.2),
     'L1_xattn_ln_mlp_offset': (0.0, 0.349),
     'L1_xattn_b_fc1': (0.0, 0.1),
     'L1_xattn_b_fc2': (0.0, 0.1)}
    factors = {'L0_xattn_w_q': 2.946,
     'L0_xattn_w_k': 3.037,
     'L1_xattn_wq1': 3.904,
     'L1_xattn_wk1': 3.82,
     'L1_xattn_bias_k1': 64.0,
     'L1_xattn_bias_v1': 64.0,
     'L1_xattn_wq2': 3.895,
     'L1_xattn_wk2': 3.818,
     'L1_xattn_bias_k2': 64.0,
     'L1_xattn_bias_v2': 64.0}
    for name, (base, spread) in spreads.items():
        noise = np.random.default_rng([zlib.crc32(name.encode()), seed]).standard_normal(out[name].shape)
        drawn = base * np.exp(spread * noise) if base else spread * noise
        out[name] = jnp.asarray(drawn.astype(out[name].dtype))
    for name, factor in factors.items():
        out[name] = (out[name] * factor).astype(out[name].dtype)
    return out
```

```python
from contextlib import ExitStack

import numpy as np

import concourse.bass as bass
from concourse import mybir

F32 = mybir.dt.float32
F32R = mybir.dt.float32r
ACT = mybir.ActivationFunctionType
ALU = mybir.AluOpType
AX_X = mybir.AxisListType.X

P = 128
B, L, D = 8, 100, 512
S = 361
T = S + 1
H = 16
DC = D // P
TOK = B * L
N = TOK // 2
NB = B // 2
CH = 121
CHUNKS = [(0, CH), (CH, CH), (2 * CH, T - 2 * CH)]
LAYERS = 2
FB = 16
EPS = 1e-5
HEAD_SCALE = float(P) ** -0.5
FULL_SCALE = float(D) ** -0.5
BQ, BK, BV, BIAS_K, BIAS_V = range(5)
WQ, WK, WV, WO = range(4)
SCALE_COL, OFFSET_COL, RES_COL = range(3)


def build(nc, xT_d, ctxT_d, ctx_d, l0w_d, alpha_d, head_w_d, head_b_d, norm_d, mlp_w_d, mlp_b_d, out_d):
    with ExitStack() as ctx:
        def sb(name, shape, dt=F32, stack=ctx):
            return stack.enter_context(nc.sbuf_tensor(name, shape, dt))

        def split(name, shape, stack=ctx):
            return sb(name + "_hi", shape, F32R, stack), sb(name + "_lo", shape, F32R, stack)

        def sem(name):
            return ctx.enter_context(nc.semaphore(name))

        ident = sb("ident", [P, P])
        mean_w = sb("mean_w", [P, P])
        zero_col = sb("zero_col", [P, 1])
        eps_col = sb("eps_col", [P, 1])
        alpha_col = sb("alpha_col", [P, 1])
        stats = sb("stats", [P, 2, 4])
        norm_p = sb("norm_p", [P, DC, 3])
        head_b = sb("head_b", [P, 2, 5])
        xT = sb("xT", [P, DC, TOK])
        h_hi, h_lo = split("h", [P, DC, TOK])
        c_hi, c_lo = split("ctxT", [P, DC, B * T])

        with ExitStack() as first:
            qk_hi, qk_lo = split("w_qk", [P, DC, D], first)
            vo_hi, vo_lo = split("w_vo", [P, DC, D], first)
            ctx_stage = sb("ctx_stage", [P, DC, S], F32, first)
            with ExitStack() as raw:
                l0w = [sb(f"l0w{j}", [P, DC, D], F32, raw) for j in range(4)]
            q2_hi, q2_lo = split("q2", [P, DC, TOK], first)
            ctx_rows = sb("ctx_rows", [P, 2, 3, D], F32, first)
            prob0 = sb("prob0", [P, S], F32, first)
            probT0 = sb("probT0", [P, 3, L], F32, first)

        stage = sb("stage", [P, 4, D])
        wq_hi, wq_lo = split("wq", [P, D])
        wk_hi, wk_lo = split("wk", [P, 2, D])
        wv_hi, wv_lo = split("wv", [P, 2, D])
        wo_hi, wo_lo = split("wo", [P, 2, D])
        with ExitStack() as norm:
            cen = sb("cen", [P, 2, DC, N], F32, norm)
            sq = sb("sq", [P, 2, DC, N], F32, norm)
            rstd = sb("rstd", [P, 2, N], F32, norm)
        with ExitStack() as mlp:
            gelu = sb("gelu", [P, 2, N], F32, mlp)
            g_hi, g_lo = split("g", [P, 2, TOK], mlp)
        q_hi, q_lo = split("q", [P, TOK])
        k_hi, k_lo = split("k", [P, 2, T])
        vT = sb("vT", [P, 2, T])
        v_hi, v_lo = split("v", [P, 3, P])
        prob = sb("prob", [P, T])
        pT_hi, pT_lo = split("pT", [P, 3, L])
        o_hi, o_lo = split("o", [P, TOK])

        psum = ctx.enter_context(nc.psum_tensor("psum", [P, 8, 512], F32))
        bank = [psum[:, j, :] for j in range(8)]
        K_BANK, V_BANK, S_BANK, VT_BANK, PT_BANK, O_BANK, Q_BANK, Y_BANK = range(8)

        const_ready, ident0 = sem("const_ready"), sem("ident0")
        x_ld, alpha_ld, l0w_ld = sem("x_ld"), sem("alpha_ld"), [sem(f"l0w_ld{j}") for j in range(4)]
        cstage_ld, crows_ld = sem("cstage_ld"), [sem(f"crows_ld{j}") for j in range(2)]
        x_hi_s, x_lo_s, c_hi_s, c_lo_s = sem("x_hi_s"), sem("x_lo_s"), sem("c_hi_s"), sem("c_lo_s")
        lw_mm, lw_hi, lw_lo = sem("lw_mm"), sem("lw_hi"), sem("lw_lo")
        lq_mm, lq_hi, lq_lo = sem("lq_mm"), sem("lq_hi"), sem("lq_lo")
        ls_mm, ls_max, ls_neg, ls_exp, ls_rcp, ls_norm = (sem(n) for n in (
            "ls_mm", "ls_max", "ls_neg", "ls_exp", "ls_rcp", "ls_norm"))
        lp_mm, lp_ev, lu_mm, lu_hi, lu_lo, ld_mm = (sem(n) for n in (
            "lp_mm", "lp_ev", "lu_mm", "lu_hi", "lu_lo", "ld_mm"))
        norm_ld, n_mean, n_cen, n_sq, n_var, n_sd, n_rstd, n_scaled, n_full, n_hi, n_lo, n_res = (sem(n) for n in (
            "norm_ld", "n_mean", "n_cen", "n_sq", "n_var", "n_sd", "n_rstd", "n_scaled", "n_full", "n_hi", "n_lo",
            "n_res"))
        stage_ld, w_hi_s = sem("stage_ld"), sem("w_hi_s")
        bias_ld = [sem(f"bias_ld{j}") for j in range(2)]
        wk_ready, wv_ready, wq_ready, wo_ready = (sem(n) for n in ("wk_ready", "wv_ready", "wq_ready", "wo_ready"))
        col_hi, col_ready = sem("col_hi"), sem("col_ready")
        q_mm, q_hi_s, q_lo_s = sem("q_mm"), sem("q_hi_s"), sem("q_lo_s")
        k_mm, k_hi_s, k_lo_s = sem("k_mm"), sem("k_hi_s"), sem("k_lo_s")
        s_mm, s_max, s_neg, s_exp, s_rcp, s_norm = (sem(n) for n in (
            "s_mm", "s_max", "s_neg", "s_exp", "s_rcp", "s_norm"))
        v_mm, v_ev, vt_mm, v_hi_s, v_lo_s = (sem(n) for n in ("v_mm", "v_ev", "vt_mm", "v_hi_s", "v_lo_s"))
        pt_mm, pt_hi_s, pt_lo_s = sem("pt_mm"), sem("pt_hi_s"), sem("pt_lo_s")
        o_mm, o_hi_s, o_lo_s, y_mm, y_add = (sem(n) for n in ("o_mm", "o_hi_s", "o_lo_s", "y_mm", "y_add"))
        mlp_b_ld, mstage_ld = [sem(f"mlp_b_ld{j}") for j in range(2)], [sem(f"mstage_ld{j}") for j in range(2)]
        mw_hi_s, w1_ready, w2_ready = sem("mw_hi_s"), sem("w1_ready"), sem("w2_ready")
        g_mm, g_gelu, g_hi_s, g_lo_s, m_mm, m_add, out_st = (sem(n) for n in (
            "g_mm", "g_gelu", "g_hi_s", "g_lo_s", "m_mm", "m_add", "out_st"))

        HEADS, STEPS = LAYERS * H, LAYERS * H * B

        def wait(eng, s, base, local, first):
            if first and local <= 0:
                return
            eng.wait_ge(s, base + local)

        def chunk(ap, c):
            return ap[:, c * P:(c + 1) * P]

        def tokens(n):
            return slice(n * N, (n + 1) * N)

        def pairs(eng, body):
            body(0, True, False)
            with eng.Fori(1, H // 2 - 1) as pair:
                body(pair, False, False)
            body(H // 2 - 1, False, True)

        block = ctx.enter_context(nc.Block())

        @block.sync
        def _(sp):
            sp.dma_start(xT[:, :, :], xT_d).then_inc(x_ld, 16)
            sp.dma_start(alpha_col[:, :], alpha_d.partition_broadcast(P)).then_inc(alpha_ld, 16)
            for b in range(B):
                if b >= 1:
                    sp.wait_ge(c_lo_s, b)
                sp.dma_start(ctx_stage[:, :, :], ctxT_d[b]).then_inc(cstage_ld, 16)
                if b == 0:
                    sp.wait_ge(lw_mm, 8)
                if b >= 2:
                    sp.wait_ge(lu_mm, b - 1)
                sp.dma_start(ctx_rows[0:CH, b % 2, 0:2, :],
                             ctx_d[b, 0:2 * CH, :].rearrange("(t p) d -> p t d", p=CH)).then_inc(crows_ld[b % 2], 16)
                sp.dma_start(ctx_rows[0:S - 2 * CH, b % 2, 2, :], ctx_d[b, 2 * CH:S, :]).then_inc(crows_ld[b % 2], 16)

            with sp.Fori(0, LAYERS) as l:
                sp.wait_ge(y_add, l * (H * B) + 8)
                sp.dma_start(norm_p[:, :, :], norm_d[bass.ds(l, 1)].rearrange("o p c k -> (o p) c k")).then_inc(norm_ld, 16)

                def load(pair, first, last):
                    for u in range(2):
                        hb = l * H + pair * 2
                        wait(sp, wo_ready, hb, u, first)
                        sp.dma_start(stage[:, :, :], head_w_d[bass.ds(hb + u, 1)].rearrange("o p m n -> (o p) m n"))\
                          .then_inc(stage_ld, 16)
                        wait(sp, k_lo_s, hb * B, (u - 1) * B, first)
                        wait(sp, v_ev, hb * B, (u - 1) * B, first)
                        wait(sp, q_lo_s, hb * 2, (u - 1) * 2, first)
                        wait(sp, col_ready, hb * 2, (u - 1) * 2, first)
                        sp.dma_start(head_b[:, u, :], head_b_d[bass.ds(hb + u, 1)].rearrange("o p k -> (o p) k"))\
                          .then_inc(bias_ld[u], 16)
                pairs(sp, load)

            sp.wait_ge(y_add, STEPS + 8)
            sp.dma_start(norm_p[:, :, :], norm_d[LAYERS]).then_inc(norm_ld, 16)

            def load_mlp(pair, first, last):
                for u in range(2):
                    wait(sp, w2_ready, pair * 2, u - 1, first)
                    sp.dma_start(stage[:, 2 * u:2 * u + 2, :],
                                 mlp_w_d[bass.ds(pair * 2 + u, 1)].rearrange("o p m n -> (o p) m n"))\
                      .then_inc(mstage_ld[u], 16)
                    wait(sp, g_gelu, pair * 4, 2 * (u - 1), first)
                    sp.dma_start(head_b[:, u, 0:1], mlp_b_d[bass.ds(pair * 2 + u, 1)].rearrange("o p k -> (o p) k"))\
                      .then_inc(mlp_b_ld[u], 16)
            pairs(sp, load_mlp)

            for p in range(2 * DC):
                sp.wait_ge(m_add, 8 * (FB - 1) + p + 1)
                sp.dma_start(out_d[:, p % DC, tokens(p // DC)], xT[:, p % DC, tokens(p // DC)]).then_inc(out_st, 16)
            sp.wait_ge(out_st, 16 * 2 * DC)

        @block.gpsimd
        def _(pool):
            def copy(out, in_):
                return nc.gpsimd.tensor_tensor(out, in_, zero_col[:, :].broadcast_to((P, in_.shape[1])), ALU.add)

            nc.gpsimd.memset(zero_col[:, :], 0.0).then_inc(ident0, 1)
            nc.gpsimd.memset(ident[:, :], 0.0).then_inc(ident0, 1)
            pool.wait_ge(ident0, 2)
            nc.gpsimd.affine_select(out=ident[:, :], in_=ident[:, :], compare_op=ALU.not_equal, fill=1.0, base=0,
                                    pattern=[[-1, P]], channel_multiplier=1).then_inc(const_ready, 1)
            for part in (c_hi, c_lo):
                v = part[:, :, :].rearrange("p c (b t) -> p c b t", t=T)
                nc.gpsimd.memset(v[:, :, :, S].bitcast(F32), 0.0).then_inc(const_ready, 1)

            for b in range(B):
                pool.wait_ge(cstage_ld, 16 * (b + 1))
                nc.gpsimd.tensor_copy(c_hi[:, :, b * T:b * T + S], ctx_stage[:, :, :]).then_inc(c_hi_s, 1)
                pool.wait_ge(c_hi_s, b + 1)
                nc.gpsimd.tensor_tensor(c_lo[:, :, b * T:b * T + S], ctx_stage[:, :, :],
                                        c_hi[:, :, b * T:b * T + S].bitcast(F32), ALU.subtract).then_inc(c_lo_s, 1)

            with pool.Fori(0, LAYERS) as l:
                def split_head(pair, first, last):
                    for u in range(2):
                        hb = l * H + pair * 2
                        pool.wait_ge(stage_ld, (hb + u + 1) * 16)
                        order = ((WK, wk_hi[:, u, :], wk_lo[:, u, :], wk_ready, k_mm, hb * B, (u - 1) * B),
                                 (WV, wv_hi[:, u, :], wv_lo[:, u, :], wv_ready, v_mm, hb * B, (u - 1) * B),
                                 (WQ, wq_hi[:, :], wq_lo[:, :], wq_ready, q_mm, hb * 2, u * 2),
                                 (WO, wo_hi[:, u, :], wo_lo[:, u, :], wo_ready, y_mm, hb * B, (u - 1) * B))
                        for n, (m, hi, lo, ready, user, base, local) in enumerate(order):
                            wait(pool, user, base, local, first)
                            copy(hi, stage[:, m, :]).then_inc(w_hi_s, 1)
                            pool.wait_ge(w_hi_s, hb * 4 + (4 * u + n + 1))
                            nc.gpsimd.tensor_tensor(lo, stage[:, m, :], hi.bitcast(F32), ALU.subtract)\
                              .then_inc(ready, 1)
                        pool.wait_ge(bias_ld[u], hb * 8 + 16)
                        if first and u == 0:
                            pool.wait_ge(n_lo, l * 2 + 2)
                        for j in range(2):
                            wait(pool, s_mm, hb * B, u * B - 1 + j, first)
                            wait(pool, vt_mm, hb * B, u * B - 1 + j, first)
                            copy(k_hi[:, j, S:T], head_b[:, u, BIAS_K:BIAS_K + 1]).then_inc(col_hi, 1)
                            copy(vT[:, j, S:T], head_b[:, u, BIAS_V:BIAS_V + 1])
                            pool.wait_ge(col_hi, hb * 2 + (2 * u + j + 1))
                            nc.gpsimd.tensor_tensor(k_lo[:, j, S:T], head_b[:, u, BIAS_K:BIAS_K + 1],
                                                    k_hi[:, j, S:T].bitcast(F32), ALU.subtract).then_inc(col_ready, 1)
                pool.wait_ge(y_add, l * (H * B) + 8)
                pairs(pool, split_head)

            pool.wait_ge(y_add, STEPS + 8)

            def split_mlp(pair, first, last):
                for u in range(2):
                    pool.wait_ge(mstage_ld[u], (pair + 1) * 16)
                    for n, (hi, lo, ready, user, local) in enumerate((
                            (wk_hi[:, u, :], wk_lo[:, u, :], w1_ready, g_mm, (u - 1) * 2),
                            (wo_hi[:, u, :], wo_lo[:, u, :], w2_ready, m_mm, (u - 1) * 8))):
                        wait(pool, user, pair * (4 if n == 0 else 16), local, first)
                        copy(hi, stage[:, 2 * u + n, :]).then_inc(mw_hi_s, 1)
                        pool.wait_ge(mw_hi_s, pair * 4 + (2 * u + n + 1))
                        nc.gpsimd.tensor_tensor(lo, stage[:, 2 * u + n, :], hi.bitcast(F32), ALU.subtract)\
                          .then_inc(ready, 1)
            pairs(pool, split_mlp)

        @block.tensor
        def _(pe):
            def mm3(out, w_hi, w_lo, r_hi, r_lo, start=True, stop=True):
                pe.matmul(out, w_hi, r_hi, start=start, stop=False)
                pe.matmul(out, w_hi, r_lo, start=False, stop=False)
                return pe.matmul(out, w_lo, r_hi, start=False, stop=stop)

            for g in range(8):
                left, right = (0, 1) if g < DC else (2, 3)
                pe.wait_ge(l0w_ld[left], 16)
                pe.wait_ge(l0w_ld[right], 16)
                for c in range(DC):
                    mm = pe.matmul(bank[g], chunk(l0w[left][:, c, :], g % DC), l0w[right][:, c, :],
                                   start=(c == 0), stop=(c == DC - 1))
                mm.then_inc(lw_mm, 1)
            pe.wait_ge(x_lo_s, 1)
            for g in range(8):
                n, m = g // DC, g % DC
                pe.wait_ge(lw_lo, max(DC, g + 1))
                for c in range(DC):
                    mm = mm3(bank[g][:, 0:N], chunk(qk_hi[:, c, :], m), chunk(qk_lo[:, c, :], m),
                             h_hi[:, c, tokens(n)], h_lo[:, c, tokens(n)], start=(c == 0), stop=(c == DC - 1))
                mm.then_inc(lq_mm, 1)

            def scores0(b):
                pe.wait_ge(c_lo_s, b + 1)
                pe.wait_ge(const_ready, 3)
                pe.wait_ge(lq_lo, 8)
                if b >= 2:
                    pe.wait_ge(ls_exp, b - 1)
                qs = slice(b * L, (b + 1) * L)
                for c in range(DC):
                    mm = mm3(bank[b % 2][0:L, 0:T], q2_hi[:, c, qs], q2_lo[:, c, qs],
                             c_hi[:, c, b * T:(b + 1) * T], c_lo[:, c, b * T:(b + 1) * T],
                             start=(c == 0), stop=(c == DC - 1))
                mm.then_inc(ls_mm, 1)

            scores0(0)
            for b in range(B):
                if b + 1 < B:
                    scores0(b + 1)
                pe.wait_ge(ls_norm, b + 1)
                if b >= 1:
                    pe.wait_ge(lp_ev, b)
                for t, (t0, _) in enumerate(CHUNKS):
                    rows = min(CH, S - t0)
                    mm = pe.transpose(bank[2][0:rows, t * L:(t + 1) * L], prob0[0:L, t0:t0 + rows], ident[0:L, 0:L])
                mm.then_inc(lp_mm, 1)
                pe.wait_ge(lp_ev, b + 1)
                pe.wait_ge(crows_ld[b % 2], 32 * (b // 2 + 1))
                if b >= 1:
                    pe.wait_ge(lu_lo, b)
                for m in range(DC):
                    for t, (t0, _) in enumerate(CHUNKS):
                        rows = min(CH, S - t0)
                        mm = pe.matmul(bank[3][:, m * L:(m + 1) * L], chunk(ctx_rows[0:rows, b % 2, t, :], m),
                                       probT0[0:rows, t, :], start=(t == 0), stop=(t == 2))
                mm.then_inc(lu_mm, 1)
            for g in range(8):
                n, m = g // DC, g % DC
                pe.wait_ge(lu_lo, NB * (n + 1))
                if g >= 4:
                    pe.wait_ge(y_add, g - 3)
                for c in range(DC):
                    mm = mm3(bank[4 + g % 4][:, 0:N], chunk(vo_hi[:, c, :], m), chunk(vo_lo[:, c, :], m),
                             h_hi[:, c, tokens(n)], h_lo[:, c, tokens(n)], start=(c == 0), stop=(c == DC - 1))
                mm.then_inc(ld_mm, 1)

            def norm_sums(l):
                for n in range(2):
                    for c in range(DC):
                        mm = pe.matmul(bank[n][:, 0:N], mean_w[:, :], xT[:, c, tokens(n)], start=(c == 0),
                                       stop=(c == DC - 1))
                    mm.then_inc(n_mean, 1)
                for n in range(2):
                    pe.wait_ge(n_sq, l * 2 + n + 1)
                    for c in range(DC):
                        mm = pe.matmul(bank[2 + n][:, 0:N], mean_w[:, :], sq[:, n, c, :], start=(c == 0),
                                       stop=(c == DC - 1))
                    mm.then_inc(n_var, 1)

            with pe.Fori(0, LAYERS) as l:
                pe.wait_ge(y_add, l * (H * B) + 8)
                norm_sums(l)
                pe.wait_ge(n_lo, l * 2 + 2)

                def queries(hb, h, n, u_first):
                    wait(pe, q_lo_s, hb * 2, 2 * h + n, u_first)
                    if n == 0:
                        pe.wait_ge(wq_ready, hb + (h + 1))
                    for c in range(DC):
                        mm = mm3(bank[Q_BANK][:, 0:N], chunk(wq_hi, c), chunk(wq_lo, c),
                                 h_hi[:, c, tokens(n)], h_lo[:, c, tokens(n)], start=(c == 0), stop=(c == DC - 1))
                    mm.then_inc(q_mm, 1)

                def scores(hb, sb_, i, first):
                    u, b = divmod(i, B)
                    pe.wait_ge(k_lo_s, sb_ + (i + 1))
                    if b < 2:
                        pe.wait_ge(col_ready, hb * 2 + (2 * u + b + 1))
                    if b % NB == 0:
                        pe.wait_ge(q_lo_s, hb * 2 + (2 * u + b // NB + 1))
                    wait(pe, s_exp, sb_, i, first)
                    pe_s = mm3(bank[S_BANK][0:L, 0:T], q_hi[:, b * L:(b + 1) * L], q_lo[:, b * L:(b + 1) * L],
                               k_hi[:, i % 2, :], k_lo[:, i % 2, :])
                    pe_s.then_inc(s_mm, 1)

                def attend(sb_, i, first):
                    pe.wait_ge(v_lo_s, sb_ + (i + 1))
                    pe.wait_ge(pt_lo_s, sb_ + (i + 1))
                    wait(pe, o_lo_s, sb_, i, first)
                    for t, (_, rows) in enumerate(CHUNKS):
                        mm = mm3(bank[O_BANK][:, 0:L], v_hi[0:rows, t, :], v_lo[0:rows, t, :],
                                 pT_hi[0:rows, t, :], pT_lo[0:rows, t, :], start=(t == 0), stop=(t == 2))
                    mm.then_inc(o_mm, 1)

                def project(hb, sb_, j, first):
                    u, p = divmod(j, B)
                    if p % NB == 0:
                        pe.wait_ge(o_lo_s, sb_ + (B * u + p + NB))
                    if p == 0:
                        pe.wait_ge(wo_ready, hb + (u + 1))
                    wait(pe, y_add, sb_ + 8, j, first)
                    n, m = divmod(p, DC)
                    mm3(bank[Y_BANK][:, 0:N], chunk(wo_hi[:, u % 2, :], m), chunk(wo_lo[:, u % 2, :], m),
                        o_hi[:, tokens(n)], o_lo[:, tokens(n)]).then_inc(y_mm, 1)

                def v_rows(hb, sb_, i, first):
                    u, b = divmod(i, B)
                    pe.wait_ge(v_ev, sb_ + (i + 1))
                    if b < 2:
                        pe.wait_ge(col_ready, hb * 2 + (2 * u + b + 1))
                    wait(pe, v_lo_s, sb_, i, first)
                    for t, (t0, rows) in enumerate(CHUNKS):
                        mm = pe.transpose(bank[VT_BANK][0:rows, t * P:(t + 1) * P], vT[:, i % 2, t0:t0 + rows],
                                          ident[:, :])
                    mm.then_inc(vt_mm, 1)

                def prob_rows(sb_, i, first):
                    pe.wait_ge(s_norm, sb_ + (i + 1))
                    wait(pe, pt_lo_s, sb_, i, first)
                    for t, (t0, rows) in enumerate(CHUNKS):
                        mm = pe.transpose(bank[PT_BANK][0:rows, t * L:(t + 1) * L], prob[0:L, t0:t0 + rows],
                                          ident[0:L, 0:L])
                    mm.then_inc(pt_mm, 1)

                def pair_steps(pair, first, last):
                    hb = l * H + pair * 2
                    sb_ = hb * B
                    for i in range(2 * B):
                        u, b = divmod(i, B)
                        ctx_b = slice(b * T, (b + 1) * T)
                        if b == 0:
                            pe.wait_ge(wk_ready, hb + (u + 1))
                        wait(pe, k_lo_s, sb_, i, first)
                        for c in range(DC):
                            mm = mm3(bank[K_BANK][:, 0:T], chunk(wk_hi[:, u, :], c), chunk(wk_lo[:, u, :], c),
                                     c_hi[:, c, ctx_b], c_lo[:, c, ctx_b], start=(c == 0), stop=(c == DC - 1))
                        mm.then_inc(k_mm, 1)
                        if not first or i >= 1:
                            scores(*shift(hb, sb_, i - 1, first))
                        if not first or i >= 2:
                            attend(*shift(hb, sb_, i - 2, first)[1:])
                        if b == 0:
                            pe.wait_ge(wv_ready, hb + (u + 1))
                        wait(pe, v_ev, sb_, i, first)
                        for c in range(DC):
                            mm = mm3(bank[V_BANK][:, 0:T], chunk(wv_hi[:, u, :], c), chunk(wv_lo[:, u, :], c),
                                     c_hi[:, c, ctx_b], c_lo[:, c, ctx_b], start=(c == 0), stop=(c == DC - 1))
                        mm.then_inc(v_mm, 1)
                        if b == 2:
                            queries(hb, u, 1, first)
                        if b == 5 and not (last and u == 1):
                            queries(hb, u + 1, 0, first)
                        if not first or i >= 6:
                            project(*shift(hb, sb_, i - 6, first))
                        if not first or i >= 1:
                            v_rows(*shift(hb, sb_, i - 1, first))
                            prob_rows(*shift(hb, sb_, i - 1, first)[1:])

                def shift(hb, sb_, i, first):
                    if i >= 0:
                        return hb, sb_, i, first
                    return hb - 2, sb_ - 2 * B, i + 2 * B, False

                queries(l * H, 0, 0, True)
                pairs(pe, pair_steps)
                hb = l * H + (H - 2)
                sb_ = hb * B
                scores(hb, sb_, 15, False)
                attend(sb_, 14, False)
                v_rows(hb, sb_, 15, False)
                project(hb, sb_, 10, False)
                prob_rows(sb_, 15, False)
                project(hb, sb_, 11, False)
                attend(sb_, 15, False)
                for j in range(12, 16):
                    project(hb, sb_, j, False)

            pe.wait_ge(y_add, STEPS + 8)
            norm_sums(LAYERS)
            pe.wait_ge(n_lo, LAYERS * 2 + 2)

            def hidden(fb, f, first):
                pe.wait_ge(w1_ready, fb + (f + 1))
                for n in range(2):
                    wait(pe, g_gelu, fb * 2, 2 * f + n - 1, first)
                    for c in range(DC):
                        mm = mm3(bank[n][:, 0:N], chunk(wk_hi[:, f % 2, :], c), chunk(wk_lo[:, f % 2, :], c),
                                 h_hi[:, c, tokens(n)], h_lo[:, c, tokens(n)], start=(c == 0), stop=(c == DC - 1))
                    mm.then_inc(g_mm, 1)

            def mlp_steps(pair, first, last):
                fb = pair * 2
                for u in range(2):
                    if not (last and u == 1):
                        hidden(fb, u + 1, first)
                    pe.wait_ge(w2_ready, fb + (u + 1))
                    for p in range(8):
                        n, m = divmod(p, DC)
                        if m == 0:
                            pe.wait_ge(g_lo_s, fb * 2 + (2 * u + n + 1))
                        wait(pe, m_add, fb * 8, 8 * u + p - 3, first)
                        mm3(bank[4 + p % 4][:, 0:N], chunk(wo_hi[:, u, :], m), chunk(wo_lo[:, u, :], m),
                            g_hi[:, u, tokens(n)], g_lo[:, u, tokens(n)]).then_inc(m_mm, 1)

            hidden(0, 0, True)
            pairs(pe, mlp_steps)

        @block.scalar
        def _(act):
            for j in range(4):
                act.dma_start(l0w[j][:, :, :], l0w_d[j]).then_inc(l0w_ld[j], 16)
            act.wait_ge(x_ld, 16)
            nc.scalar.activation(h_hi[:, :, :], xT[:, :, :], ACT.Copy).then_inc(x_hi_s, 1)
            for g in range(8):
                act.wait_ge(lw_mm, g + 1)
                dst = qk_hi if g < DC else vo_hi
                nc.scalar.activation(dst[:, g % DC, :], bank[g], ACT.Copy).then_inc(lw_hi, 1)
            for g in range(8):
                n, m = divmod(g, DC)
                act.wait_ge(lq_mm, g + 1)
                nc.scalar.activation(q2_hi[:, m, tokens(n)], bank[g][:, 0:N], ACT.Copy).then_inc(lq_hi, 1)
            for b in range(B):
                act.wait_ge(ls_neg, b + 1)
                if b >= 1:
                    act.wait_ge(lp_mm, b)
                st = stats[0:L, b % 2, :]
                nc.scalar.activation(prob0[0:L, :], bank[b % 2][0:L, 0:S], ACT.Exp, bias=st[:, 1:2], scale=FULL_SCALE,
                                     accum_out=st[:, 2:3]).then_inc(ls_exp, 1)
                act.wait_ge(lp_mm, b + 1)
                if b >= 1:
                    act.wait_ge(lu_mm, b)
                nc.scalar.activation(probT0[0:CH, 0:2, :], bank[2][0:CH, 0:2 * L].rearrange("p (t q) -> p t q", q=L),
                                     ACT.Copy)
                nc.scalar.activation(probT0[0:S - 2 * CH, 2, :], bank[2][0:S - 2 * CH, 2 * L:3 * L],
                                     ACT.Copy).then_inc(lp_ev, 1)
                act.wait_ge(lu_mm, b + 1)
                nc.scalar.activation(h_hi[:, :, b * L:(b + 1) * L],
                                     bank[3][:, 0:DC * L].rearrange("p (m q) -> p m q", q=L),
                                     ACT.Copy).then_inc(lu_hi, 1)

            def norm_act(l):
                for n in range(2):
                    act.wait_ge(n_cen, l * 2 + n + 1)
                    nc.scalar.activation(sq[:, n, :, :], cen[:, n, :, :], ACT.Square).then_inc(n_sq, 1)
                for n in range(2):
                    act.wait_ge(n_var, l * 2 + n + 1)
                    nc.scalar.activation(rstd[:, n, :], bank[2 + n][:, 0:N], ACT.Sqrt, bias=eps_col[:, :])\
                      .then_inc(n_sd, 1)
                for n in range(2):
                    act.wait_ge(n_full, l * 2 + n + 1)
                    nc.scalar.activation(h_hi[:, :, tokens(n)], cen[:, n, :, :], ACT.Copy).then_inc(n_hi, 1)

            act.wait_ge(const_ready, 5)
            with act.Fori(0, LAYERS) as l:
                norm_act(l)
                act.wait_ge(n_lo, l * 2 + 2)

                def queries_hi(hb, h, n, first):
                    act.wait_ge(q_mm, hb * 2 + (2 * h + n + 1))
                    if n == 0:
                        act.wait_ge(bias_ld[h % 2], (hb + 2 * (h // 2)) * 8 + 16)
                    wait(act, s_mm, hb * B, B * (h - 1) + NB * (n + 1), first)
                    nc.scalar.activation(q_hi[:, tokens(n)], bank[Q_BANK][:, 0:N], ACT.Identity,
                                         bias=head_b[:, h % 2, BQ:BQ + 1]).then_inc(q_hi_s, 1)

                def exps(sb_, i, first):
                    act.wait_ge(s_neg, sb_ + (i + 1))
                    wait(act, pt_mm, sb_, i, first)
                    st = stats[0:L, i % 2, :]
                    nc.scalar.activation(prob[0:L, :], bank[S_BANK][0:L, 0:T], ACT.Exp, bias=st[:, 1:2],
                                         scale=HEAD_SCALE, accum_out=st[:, 2:3]).then_inc(s_exp, 1)

                def rows_hi(sb_, i, first):
                    act.wait_ge(vt_mm, sb_ + (i + 1))
                    wait(act, o_mm, sb_, i, first)
                    nc.scalar.activation(v_hi[0:CH, :, :].rearrange("p t k -> p (t k)"), bank[VT_BANK][0:CH, 0:3 * P],
                                         ACT.Copy).then_inc(v_hi_s, 1)
                    act.wait_ge(pt_mm, sb_ + (i + 1))
                    nc.scalar.activation(pT_hi[0:CH, :, :].rearrange("p t k -> p (t k)"), bank[PT_BANK][0:CH, 0:3 * L],
                                         ACT.Copy).then_inc(pt_hi_s, 1)

                def shift(sb_, i, first):
                    return (sb_, i, first) if i >= 0 else (sb_ - 2 * B, i + 2 * B, False)

                def pair_steps(pair, first, last):
                    hb = l * H + pair * 2
                    sb_ = hb * B
                    for i in range(2 * B):
                        u, b = divmod(i, B)
                        act.wait_ge(k_mm, sb_ + (i + 1))
                        if b == 0:
                            act.wait_ge(bias_ld[u], hb * 8 + 16)
                        wait(act, s_mm, sb_, i - 1, first)
                        nc.scalar.activation(k_hi[:, i % 2, 0:S], bank[K_BANK][:, 0:S], ACT.Identity,
                                             bias=head_b[:, u, BK:BK + 1]).then_inc(k_hi_s, 1)
                        if not first or i >= 1:
                            exps(*shift(sb_, i - 1, first))
                        act.wait_ge(v_mm, sb_ + (i + 1))
                        wait(act, vt_mm, sb_, i - 1, first)
                        nc.scalar.activation(vT[:, i % 2, 0:S], bank[V_BANK][:, 0:S], ACT.Identity,
                                             bias=head_b[:, u, BV:BV + 1]).then_inc(v_ev, 1)
                        if b == 2:
                            queries_hi(hb, u, 1, first)
                        if b == 5 and not (last and u == 1):
                            queries_hi(hb, u + 1, 0, first)
                        if not first or i >= 1:
                            rows_hi(*shift(sb_, i - 1, first))

                queries_hi(l * H, 0, 0, True)
                pairs(act, pair_steps)
                sb_ = (l * H + (H - 2)) * B
                exps(sb_, 15, False)
                rows_hi(sb_, 15, False)

            norm_act(LAYERS)
            act.wait_ge(n_lo, LAYERS * 2 + 2)

            def mlp_act(pair, first, last):
                for u in range(2):
                    for n in range(2):
                        act.wait_ge(g_mm, pair * 4 + (2 * u + n + 1))
                        wait(act, g_lo_s, pair * 4, 2 * u + n - 1, first)
                        if n == 0:
                            act.wait_ge(mlp_b_ld[u], pair * 16 + 16)
                        nc.scalar.activation(gelu[:, n, :], bank[n][:, 0:N], ACT.Gelu, bias=head_b[:, u, 0:1]).then_inc(g_gelu, 1)
                        act.wait_ge(g_gelu, pair * 4 + (2 * u + n + 1))
                        wait(act, m_mm, pair * 16, 8 * (u - 1), first)
                        nc.scalar.activation(g_hi[:, u, tokens(n)], gelu[:, n, :], ACT.Copy).then_inc(g_hi_s, 1)
            pairs(act, mlp_act)

        @block.vector
        def _(dve):
            dve_sub = ALU.subtract
            nc.vector.memset(mean_w[:, :], 1.0 / D).then_inc(const_ready, 1)
            nc.vector.memset(eps_col[:, :], EPS).then_inc(const_ready, 1)
            dve.wait_ge(x_hi_s, 1)
            nc.vector.tensor_tensor(h_lo[:, :, :], xT[:, :, :], h_hi[:, :, :].bitcast(F32), dve_sub).then_inc(x_lo_s, 1)
            for g in range(8):
                hi, lo = (qk_hi, qk_lo) if g < DC else (vo_hi, vo_lo)
                dve.wait_ge(lw_hi, g + 1)
                nc.vector.tensor_tensor(lo[:, g % DC, :], bank[g], hi[:, g % DC, :].bitcast(F32), dve_sub)\
                  .then_inc(lw_lo, 1)
            for g in range(8):
                n, m = divmod(g, DC)
                dve.wait_ge(lq_hi, g + 1)
                nc.vector.tensor_tensor(q2_lo[:, m, tokens(n)], bank[g][:, 0:N], q2_hi[:, m, tokens(n)].bitcast(F32),
                                        dve_sub).then_inc(lq_lo, 1)

            def max0(b):
                st = stats[0:L, b % 2, :]
                dve.wait_ge(ls_mm, b + 1)
                nc.vector.reduce_max(st[:, 0:1], bank[b % 2][0:L, 0:S], AX_X).then_inc(ls_max, 1)
                dve.wait_ge(ls_max, b + 1)
                nc.vector.tensor_scalar(st[:, 1:2], st[:, 0:1], -FULL_SCALE, None, ALU.mult).then_inc(ls_neg, 1)

            max0(0)
            for b in range(B):
                st = stats[0:L, b % 2, :]
                dve.wait_ge(ls_exp, b + 1)
                nc.vector.reciprocal(st[:, 3:4], st[:, 2:3]).then_inc(ls_rcp, 1)
                dve.wait_ge(ls_rcp, b + 1)
                nc.vector.tensor_scalar(prob0[0:L, :], prob0[0:L, :], st[:, 3:4], None, ALU.mult).then_inc(ls_norm, 1)
                if b + 1 < B:
                    max0(b + 1)
                dve.wait_ge(lu_hi, b + 1)
                qs = slice(b * L, (b + 1) * L)
                nc.vector.tensor_tensor(h_lo[:, :, qs], bank[3][:, 0:DC * L].rearrange("p (m q) -> p m q", q=L),
                                        h_hi[:, :, qs].bitcast(F32), dve_sub).then_inc(lu_lo, 1)
            dve.wait_ge(alpha_ld, 16)
            for g in range(8):
                n, m = divmod(g, DC)
                dve.wait_ge(ld_mm, g + 1)
                nc.vector.scalar_tensor_tensor(out=xT[:, m, tokens(n)], in0=bank[4 + g % 4][:, 0:N],
                                               scalar=alpha_col[:, 0:1], in1=xT[:, m, tokens(n)], op0=ALU.mult,
                                               op1=ALU.add).then_inc(y_add, 1)

            def norm_dve(l):
                for n in range(2):
                    dve.wait_ge(n_mean, l * 2 + n + 1)
                    mean = bank[n][:, 0:N].unsqueeze(1).broadcast_to((P, DC, N))
                    nc.vector.tensor_tensor(cen[:, n, :, :], xT[:, :, tokens(n)], mean, dve_sub).then_inc(n_cen, 1)
                dve.wait_ge(norm_ld, (l + 1) * 16)
                dve.wait_ge(n_cen, l * 2 + 2)
                for c in range(DC):
                    r = nc.vector.tensor_scalar(xT[:, c, :], xT[:, c, :], norm_p[:, c, RES_COL:RES_COL + 1], None,
                                                ALU.add)
                r.then_inc(n_res, 1)
                for n in range(2):
                    dve.wait_ge(n_sd, l * 2 + n + 1)
                    nc.vector.reciprocal(rstd[:, n, :], rstd[:, n, :]).then_inc(n_rstd, 1)
                    dve.wait_ge(n_rstd, l * 2 + n + 1)
                    r = rstd[:, n, :].unsqueeze(1).broadcast_to((P, DC, N))
                    nc.vector.tensor_tensor(cen[:, n, :, :], cen[:, n, :, :], r, ALU.mult).then_inc(n_scaled, 1)
                    dve.wait_ge(n_scaled, l * 2 + n + 1)
                    for c in range(DC):
                        f = nc.vector.tensor_scalar(cen[:, n, c, :], cen[:, n, c, :],
                                                    norm_p[:, c, SCALE_COL:SCALE_COL + 1],
                                                    norm_p[:, c, OFFSET_COL:OFFSET_COL + 1], ALU.mult, ALU.add)
                    f.then_inc(n_full, 1)
                for n in range(2):
                    dve.wait_ge(n_hi, l * 2 + n + 1)
                    nc.vector.tensor_tensor(h_lo[:, :, tokens(n)], cen[:, n, :, :],
                                            h_hi[:, :, tokens(n)].bitcast(F32), dve_sub).then_inc(n_lo, 1)

            dve.wait_ge(y_add, 8)
            with dve.Fori(0, LAYERS) as l:
                norm_dve(l)

                def queries_lo(hb, h, n):
                    dve.wait_ge(q_hi_s, hb * 2 + (2 * h + n + 1))
                    nc.vector.scalar_tensor_tensor(out=q_lo[:, tokens(n)], in0=bank[Q_BANK][:, 0:N],
                                                   scalar=head_b[:, h % 2, BQ:BQ + 1],
                                                   in1=q_hi[:, tokens(n)].bitcast(F32), op0=ALU.add, op1=dve_sub)\
                      .then_inc(q_lo_s, 1)

                def maxima(sb_, i):
                    st = stats[0:L, i % 2, :]
                    dve.wait_ge(s_mm, sb_ + (i + 1))
                    nc.vector.reduce_max(st[:, 0:1], bank[S_BANK][0:L, 0:T], AX_X).then_inc(s_max, 1)
                    dve.wait_ge(s_max, sb_ + (i + 1))
                    nc.vector.tensor_scalar(st[:, 1:2], st[:, 0:1], -HEAD_SCALE, None, ALU.mult).then_inc(s_neg, 1)

                def normalise(sb_, i):
                    st = stats[0:L, i % 2, :]
                    dve.wait_ge(s_exp, sb_ + (i + 1))
                    nc.vector.reciprocal(st[:, 3:4], st[:, 2:3]).then_inc(s_rcp, 1)
                    dve.wait_ge(s_rcp, sb_ + (i + 1))
                    nc.vector.tensor_scalar(prob[0:L, :], prob[0:L, :], st[:, 3:4], None, ALU.mult)\
                      .then_inc(s_norm, 1)

                def attended(sb_, i, first):
                    u, b = divmod(i, B)
                    qs = slice(b * L, (b + 1) * L)
                    dve.wait_ge(o_mm, sb_ + (i + 1))
                    if b % NB == 0:
                        wait(dve, y_mm, sb_, B * u + b - NB, first)
                    nc.vector.tensor_copy(o_hi[:, qs], bank[O_BANK][:, 0:L]).then_inc(o_hi_s, 1)
                    dve.wait_ge(o_hi_s, sb_ + (i + 1))
                    nc.vector.tensor_tensor(o_lo[:, qs], bank[O_BANK][:, 0:L], o_hi[:, qs].bitcast(F32), dve_sub)\
                      .then_inc(o_lo_s, 1)

                def add_piece(sb_, j):
                    n, m = divmod(j % B, DC)
                    dve.wait_ge(y_mm, sb_ + (j + 1))
                    nc.vector.tensor_tensor(xT[:, m, tokens(n)], bank[Y_BANK][:, 0:N], xT[:, m, tokens(n)], ALU.add)\
                      .then_inc(y_add, 1)

                def rows_lo(sb_, i):
                    dve.wait_ge(v_hi_s, sb_ + (i + 1))
                    nc.vector.tensor_tensor(v_lo[0:CH, :, :].rearrange("p t k -> p (t k)"), bank[VT_BANK][0:CH, 0:3 * P],
                                            v_hi[0:CH, :, :].rearrange("p t k -> p (t k)").bitcast(F32), dve_sub)\
                      .then_inc(v_lo_s, 1)
                    dve.wait_ge(pt_hi_s, sb_ + (i + 1))
                    nc.vector.tensor_tensor(pT_lo[0:CH, :, :].rearrange("p t k -> p (t k)"), bank[PT_BANK][0:CH, 0:3 * L],
                                            pT_hi[0:CH, :, :].rearrange("p t k -> p (t k)").bitcast(F32), dve_sub)\
                      .then_inc(pt_lo_s, 1)

                def shift(sb_, i, first):
                    return (sb_, i, first) if i >= 0 else (sb_ - 2 * B, i + 2 * B, False)

                def pair_steps(pair, first, last):
                    hb = l * H + pair * 2
                    sb_ = hb * B
                    for i in range(2 * B):
                        u, b = divmod(i, B)
                        dve.wait_ge(k_hi_s, sb_ + (i + 1))
                        nc.vector.scalar_tensor_tensor(out=k_lo[:, i % 2, 0:S], in0=bank[K_BANK][:, 0:S],
                                                       scalar=head_b[:, u, BK:BK + 1],
                                                       in1=k_hi[:, i % 2, 0:S].bitcast(F32), op0=ALU.add, op1=dve_sub)\
                          .then_inc(k_lo_s, 1)
                        if not first or i >= 1:
                            maxima(*shift(sb_, i - 1, first)[:2])
                        if not first or i >= 2:
                            attended(*shift(sb_, i - 2, first))
                        if not first or i >= 1:
                            normalise(*shift(sb_, i - 1, first)[:2])
                        if b == 2:
                            queries_lo(hb, u, 1)
                        if b == 5 and not (last and u == 1):
                            queries_lo(hb, u + 1, 0)
                        if not first or i >= 6:
                            add_piece(*shift(sb_, i - 6, first)[:2])
                        if not first or i >= 1:
                            rows_lo(*shift(sb_, i - 1, first)[:2])

                queries_lo(l * H, 0, 0)
                pairs(dve, pair_steps)
                sb_ = (l * H + (H - 2)) * B
                maxima(sb_, 15)
                attended(sb_, 14, False)
                normalise(sb_, 15)
                add_piece(sb_, 10)
                rows_lo(sb_, 15)
                add_piece(sb_, 11)
                attended(sb_, 15, False)
                for j in range(12, 16):
                    add_piece(sb_, j)

            norm_dve(LAYERS)

            def mlp_dve(pair, first, last):
                def gate_lo(u, n):
                    dve.wait_ge(g_hi_s, pair * 4 + (2 * u + n + 1))
                    nc.vector.tensor_tensor(g_lo[:, u % 2, tokens(n)], gelu[:, n, :],
                                            g_hi[:, u % 2, tokens(n)].bitcast(F32), dve_sub).then_inc(g_lo_s, 1)

                for u in range(2):
                    if first and u == 0:
                        gate_lo(0, 0)
                        gate_lo(0, 1)
                    if not (last and u == 1):
                        gate_lo(u + 1, 0)
                        gate_lo(u + 1, 1)
                    for p in range(8):
                        n, m = divmod(p, DC)
                        dve.wait_ge(m_mm, pair * 16 + (8 * u + p + 1))
                        nc.vector.tensor_tensor(xT[:, m, tokens(n)], bank[4 + p % 4][:, 0:N], xT[:, m, tokens(n)],
                                                ALU.add).then_inc(m_add, 1)
            pairs(dve, mlp_dve)


def kernel(**inputs):
    import concourse.bacc as _bacc
    from concourse import mybir as _mybir
    from concourse.bass_utils import run_bass_kernel_spmd as _run

    a = {k: np.asarray(v) for k, v in inputs.items()}

    def rows(m):
        return np.moveaxis(m.reshape(m.shape[:-2] + (m.shape[-2] // P, P, m.shape[-1])), -3, -2)

    def head_cols(m):
        return rows(np.moveaxis(m.reshape(D, H, P), 1, 0)).reshape(H, P, D)

    def layer_w(i):
        w = {n: a[f"L1_xattn_{n}{i}"] for n in ("wq", "wk", "wv", "wo")}
        return np.stack([head_cols(w["wq"]), head_cols(w["wk"]), head_cols(w["wv"]), w["wo"].reshape(H, P, D)], 2)

    def layer_b(i):
        names = (f"bq{i}", f"bk{i}", f"bv{i}", f"bias_k{i}", f"bias_v{i}")
        return np.stack([a[f"L1_xattn_{n}"].reshape(H, P) for n in names], 2)

    def norm_cols(*names):
        return np.stack([a[f"L1_xattn_{n}"].reshape(DC, P).T for n in names], 2)

    arrays = {
        "xT": rows(a["x"].reshape(TOK, D).T),
        "ctxT": rows(np.moveaxis(a["ctx_2048"], 1, 2)),
        "ctx_rows": a["ctx_2048"],
        "l0_w": np.stack([rows(a["L0_xattn_w_q"]), rows(a["L0_xattn_w_k"]), rows(a["L0_xattn_w_v"]),
                          rows(a["L0_xattn_w_o"].T)]),
        "alpha": a["L0_xattn_alpha"].reshape(1),
        "head_w": np.concatenate([layer_w(1), layer_w(2)]),
        "head_b": np.concatenate([layer_b(1), layer_b(2)]),
        "norm_p": np.stack([norm_cols("ln1_scale", "ln1_offset", "bo1"), norm_cols("ln2_scale", "ln2_offset", "bo2"),
                            norm_cols("ln_mlp_scale", "ln_mlp_offset", "b_fc2")]),
        "mlp_w": np.stack([head_cols(a["L1_xattn_w_fc1"]), a["L1_xattn_w_fc2"].reshape(FB, P, D)], 2),
        "mlp_b": a["L1_xattn_b_fc1"].reshape(FB, P, 1),
    }
    nc = _bacc.Bacc("TRN2", target_bir_lowering=False, num_devices=1)
    feed, args = {}, []
    for name, arr in arrays.items():
        feed[f"{name}_dram"] = np.ascontiguousarray(arr)
        args.append(nc.dram_tensor(f"{name}_dram", arr.shape, _mybir.dt.from_np(arr.dtype), kind="ExternalInput").ap())
    out = nc.dram_tensor("out_dram", (P, DC, TOK), F32, kind="ExternalOutput").ap()
    build(nc, *args, out)
    r = _run(nc, [feed], core_ids=[0])
    return np.ascontiguousarray(r.results[0]["out_dram"].transpose(2, 1, 0)).reshape(B, L, D)
```

```python
from contextlib import ExitStack

import numpy as np

import concourse.bass as bass
from concourse import mybir

F32 = mybir.dt.float32
F32R = mybir.dt.float32r
ACT = mybir.ActivationFunctionType
ALU = mybir.AluOpType
AX_X = mybir.AxisListType.X

P = 128
B, L, D = 8, 100, 512
S = 361
T = S + 1
H = 16
DC = D // P
HALVES = 2
TURNS = HALVES
NB = B // HALVES
N = NB * L
NQ = N // 2
CH = 121
CHUNKS = [(0, CH), (CH, CH), (2 * CH, T - 2 * CH)]
LAYERS = 2
PAIRS = H // 2
STEPS = 2 * NB
FB = 16
QUADS = FB // 4
EPS = 1e-5
HEAD_SCALE = float(P) ** -0.5
FULL_SCALE = float(D) ** -0.5
BQ, BK, BV, BIAS_K = range(4)
Y_BANKS = (5, 6, 3, 4, 5, 6, 7, 3)
WQ, WK, WV, WO = range(4)
SCALE_COL, OFFSET_COL, RES_COL = range(3)


def build(nc, xT_d, ctxT_d, ctx_d, l0w_d, alpha_d, pair_w_d, cols_d, rows_d, norm_d, mlp_w_d, mlp_b_d, out_d):
    with ExitStack() as ctx:
        def sb(name, shape, dt=F32, stack=ctx):
            return stack.enter_context(nc.sbuf_tensor(name, shape, dt))

        def split(name, shape, stack=ctx):
            return sb(name + "_hi", shape, F32R, stack), sb(name + "_lo", shape, F32R, stack)

        def sem(name):
            return ctx.enter_context(nc.semaphore(name))

        ident = sb("ident", [P, P])
        mean_w = sb("mean_w", [P, P])
        zero_col = sb("zero_col", [P, 1])
        eps_col = sb("eps_col", [P, 1])
        alpha_col = sb("alpha_col", [P, 1])
        flag = sb("flag", [P, 1])
        unused = sb("unused", [P, 1])
        stats = sb("stats", [P, 2, 4])
        norm_p = sb("norm_p", [P, DC, 3])
        cols = sb("cols", [P, 4, LAYERS * H])
        bq_c, bk_c, bv_c = (sb(n, [P, 2]) for n in ("bq_c", "bk_c", "bv_c"))
        mlp_b = sb("mlp_b", [P, FB])
        dv3 = sb("dv3", [65, 2 * P], F32R)
        pb3 = sb("pb3", [65, 2, N], F32R)
        mlp_b_c = sb("mlp_b_c", [P, 2])
        xT = sb("xT", [P, DC, N])
        h_hi, h_lo = split("h", [P, DC, N])
        c_hi, c_lo = split("ctxT", [P, DC, NB * T])
        r_hi, r_lo = split("ctx_rows", [P, NB * 3, D])

        with ExitStack() as before_turns:
            l0w = [sb(f"l0w{j}", [P, DC, D], F32, before_turns) for j in range(4)]
        with ExitStack() as second_turn:
            x1 = sb("x1", [P, DC, N], F32, second_turn)
            p0_hi, p0_lo = split("p0", [P, 3, L], second_turn)
            u_rows = sb("u_rows", [P, D], F32, second_turn)
            x1_hi, x1_lo = split("x1", [P, DC, N], second_turn)
        with ExitStack() as first_block:
            sb("l0w_space", [P, 4 * DC * D], F32, first_block)
            qk_hi, qk_lo = split("w_qk", [P, DC, D], first_block)
            vo_hi, vo_lo = split("w_vo", [P, DC, D], first_block)
            q2_hi, q2_lo = split("q2", [P, DC, N], first_block)
            prob0 = sb("prob0", [P, T], F32, first_block)
            ct_stage = sb("ct_stage", [P, DC, S], F32, first_block)
            cr_stage = sb("cr_stage", [P, 3, D], F32, first_block)

        with ExitStack() as mlp_only:
            more_stages = [sb(f"stage{j}", [P, 2, D], F32, mlp_only) for j in (2, 3)]
        wv_hi, wv_lo = split("wv", [P, 2, D])
        wo_hi, wo_lo = split("wo", [P, D])
        stage = [sb(f"stage{j}", [P, 2, D]) for j in range(2)]
        mlp_stage = stage + more_stages
        wq_hi, wq_lo = split("wq", [P, 2, D])
        wk_hi, wk_lo = split("wk", [P, 2, D])
        with ExitStack() as norm:
            cen = sb("cen", [P, 2, DC, NQ], F32, norm)
            sq = sb("sq", [P, 2, DC, NQ], F32, norm)
            rstd = sb("rstd", [P, 2, NQ], F32, norm)
        with ExitStack() as mlp:
            gelu = sb("gelu", [P, 2, N], F32, mlp)
            g_hi, g_lo = split("g", [P, 2, N], mlp)
            x_next = sb("x_next", [P, DC, N], F32, mlp)
            y_out = sb("y_out", [P, DC, N], F32, mlp)
            w1_hi, w1_lo = split("w1", [P, 2, D], mlp)
            w2_hi, w2_lo = split("w2", [P, 2, D], mlp)
        u_hi, u_lo = split("u", [P, DC, 2, N])
        k_hi, k_lo = split("k", [P, 2, T])
        pT_hi, pT_lo = split("pT", [P, 3, 2, L])
        prob = sb("prob", [P, T])
        q_hi, q_lo = split("q", [P, 2, N])
        dv = sb("dv", [1, 2 * P])
        o_hi, o_lo = split("o", [P, 2, N])
        vb_rows = sb("vb_rows", [1, 2, 2 * P])

        last_wo_hi, last_wo_lo = (q[:, :, :].rearrange("p u n -> p (u n)")[:, 0:D] for q in (q_hi, q_lo))

        psum = ctx.enter_context(nc.psum_tensor("psum", [P, 8, 512], F32))
        bank = [psum[:, j, :] for j in range(8)]
        K_BANK, S_BANK, PT_BANK, U_BANK, R_BANK = 0, 1, 2, 3, 5

        def sems(names):
            return [sem(n) for n in names.split()]

        const_ready, const0, x_ready = sems("const_ready const0 x_ready")
        alpha_ld, cols_ld, mlp_b_ld, ct_ld, cr_clear = sems("alpha_ld cols_ld mlp_b_ld ct_ld cr_clear")
        x_ld = [sem(f"x_ld{j}") for j in range(2)]
        xn_ld = sem("xn_ld")
        cr_ld = sem("cr_ld")
        l0w_ld = [sem(f"l0w_ld{j}") for j in range(2 * DC)]
        x_hi_s, x_lo_s, ct_hi_s, ct_lo_s, cr_hi_s, cr_lo_s = sems("x_hi_s x_lo_s ct_hi_s ct_lo_s cr_hi_s cr_lo_s")
        lw_mm, lw_hi, lw_lo, lq_mm, lq_hi, lq_lo = sems("lw_mm lw_hi lw_lo lq_mm lq_hi lq_lo")
        ls_mm, ls_max, ls_neg, ls_exp, ls_rcp, ls_norm = sems("ls_mm ls_max ls_neg ls_exp ls_rcp ls_norm")
        lp_mm, lp_hi, lp_lo, lu_mm, lu_copied, lt_mm, lu_hi, lu_lo, ld_mm = sems(
            "lp_mm lp_hi lp_lo lu_mm lu_copied lt_mm lu_hi lu_lo ld_mm")
        norm_ld, n_mean, n_cen, n_sq, n_var, n_sd, n_rstd, n_scaled, n_by_scale, n_hi, n_lo, n_res = sems(
            "norm_ld n_mean n_cen n_sq n_var n_sd n_rstd n_scaled n_by_scale n_hi n_lo n_res")
        stage_ld = [sem(f"stage_ld{j}") for j in range(2)]
        wq_hi_s, wk_hi_s, wv_hi_s, wo_hi_s = sems("wq_hi_s wk_hi_s wv_hi_s wo_hi_s")
        wq_done, wk_done, wv_done, wo_done = sems("wq_done wk_done wv_done wo_done")
        vb_ld, dv_s, dv_hi_s, dv_lo_s = sems("vb_ld dv_s dv_hi_s dv_lo_s")
        bq_ready, bk_ready, bv_ready, kcol_hi, kcol_lo = sems("bq_ready bk_ready bv_ready kcol_hi kcol_lo")
        q_mm, q_hi_s, q_lo_s, k_mm, k_hi_s, k_lo_s = sems("q_mm q_hi_s q_lo_s k_mm k_hi_s k_lo_s")
        s_mm, s_max, s_neg, s_exp, s_rcp, s_norm = sems("s_mm s_max s_neg s_exp s_rcp s_norm")
        pt_mm, pt_hi_s, pt_lo_s, pb_s, u_mm, u_hi_s, u_lo_s = sems("pt_mm pt_hi_s pt_lo_s pb_s u_mm u_hi_s u_lo_s")
        o_mm, o_hi_s, o_lo_s, y_mm, y_add = sems("o_mm o_hi_s o_lo_s y_mm y_add")
        mstage_ld = [sem(f"mstage_ld{j}") for j in range(4)]
        w1_hi_s, w2_hi_s, w1_ready, w2_ready, mlp_b_ready = sems("w1_hi_s w2_hi_s w1_ready w2_ready mlp_b_ready")
        g_mm, g_gelu, g_hi_s, g_lo_s, m_mm, m_add = sems("g_mm g_gelu g_hi_s g_lo_s m_mm m_add")
        landed = sem("landed")

        def wait(eng, s, base, local, first):
            if first and local <= 0:
                return
            eng.wait_ge(s, base + local)

        def chunk(ap, c):
            return ap[:, c * P:(c + 1) * P]

        def piece(n):
            return slice(n * NQ, (n + 1) * NQ)

        def added(half, l):
            return half * (LAYERS * PAIRS * 8) + l * (PAIRS * 8) + TURNS * DC

        def batch(b):
            return slice(b * L, (b + 1) * L)

        def ends_apart(eng, count, body):
            body(0, True, False)
            with eng.Fori(1, count - 1) as index:
                body(index, False, False)
            body(count - 1, False, True)

        def x_is(half, blocks):
            return half * (LAYERS + 1) + (blocks + 1)

        def ctx_parts(half):
            return half * NB + TURNS * NB

        def steps_before(sb_, i, first):
            return (sb_, i, first) if i >= 0 else (sb_ - STEPS, i + STEPS, False)

        block = ctx.enter_context(nc.Block())

        @block.sync
        def _(sp):
            def load_ctx(turn, b, done):
                if done is not None:
                    sp.wait_ge(ct_lo_s, done)
                sp.dma_start(ct_stage[:, :, :], ctxT_d[turn * NB + b]).then_inc(ct_ld, 16)
                if done is not None:
                    sp.wait_ge(cr_lo_s, done)
                rows = ctx_d[turn * NB + b]
                sp.dma_start(cr_stage[1:CH, 0, :], rows[0:CH - 1, :]).then_inc(cr_ld, 16)
                sp.dma_start(cr_stage[0:CH, 1, :], rows[CH - 1:2 * CH - 1, :]).then_inc(cr_ld, 16)
                sp.dma_start(cr_stage[0:CH - 1, 2, :], rows[2 * CH - 1:S, :]).then_inc(cr_ld, 16)

            sp.dma_start(xT[:, :, :], xT_d[0]).then_inc(x_ld[0], 16)
            sp.wait_ge(cr_clear, 1)
            load_ctx(0, 0, None)
            sp.dma_start(alpha_col[:, :], alpha_d.partition_broadcast(P)).then_inc(alpha_ld, 16)
            sp.dma_start(cols[:, :, :], cols_d).then_inc(cols_ld, 16)
            sp.dma_start(mlp_b[:, :], mlp_b_d).then_inc(mlp_b_ld, 16)
            for b in range(1, NB):
                load_ctx(0, b, b)
            sp.wait_ge(lw_mm, 8)
            sp.dma_start(x1[:, :, :], xT_d[1]).then_inc(x_ld[1], 16)
            for b in range(NB):
                load_ctx(1, b, NB + b)
            sp.wait_ge(y_add, DC)
            sp.dma_start(out_d[1], xT[:, :, :]).then_inc(landed, 16)

            def load(slot, w, pair_row):
                sp.dma_start(stage[slot][:, :, :],
                             pair_w_d[bass.ds(pair_row * 4 + w, 1)].rearrange("o p u n -> (o p) u n"))\
                  .then_inc(stage_ld[slot], 16)

            sp.wait_ge(lq_mm, TURNS * DC)
            load(1, WQ, 0)
            sp.wait_ge(wq_done, 2)
            load(1, WK, 0)

            with sp.Fori(0, HALVES) as half:
                with sp.Fori(0, LAYERS) as l:
                    ph = half * LAYERS + l
                    sp.wait_ge(x_ready, x_is(half, 0) + l)
                    sp.dma_start(norm_p[:, :, :], norm_d[bass.ds(l, 1)].rearrange("o p c k -> (o p) c k"))\
                      .then_inc(norm_ld, 16)

                    pg = ph * PAIRS

                    def load_wo(pair):
                        sp.wait_ge(wv_done, (pg + pair) * 2 + 2)
                        load(0, WO, l * PAIRS + pair)

                    def load_pair(pair, first, last):
                        if not first:
                            load_wo(pair - 1)
                        sp.wait_ge(wk_done, (pg + pair) * 2 + 2)
                        load(1, WQ, l * PAIRS + (pair + 1))
                        sp.wait_ge(wq_done, (pg + pair) * 2 + 4)
                        load(1, WK, l * PAIRS + (pair + 1))
                        wait(sp, wo_done, (pg + pair) * 2, 0, first)
                        load(0, WV, l * PAIRS + pair)
                        if not first:
                            sp.wait_ge(dv_s, pg + pair)
                        sp.dma_start(vb_rows[:, :, :], rows_d[bass.ds(l * PAIRS + pair, 1)]).then_inc(vb_ld, 16)
                    ends_apart(sp, PAIRS, load_pair)
                    load_wo(PAIRS - 1)

                sp.wait_ge(x_ready, x_is(half, LAYERS))
                sp.dma_start(norm_p[:, :, :], norm_d[LAYERS]).then_inc(norm_ld, 16)

                def ctx_again(b):
                    load_ctx(0, b, half * NB + (TURNS * NB + b))

                def load_mlp(quad, first, last):
                    for u in range(4):
                        if first and u == 0:
                            sp.wait_ge(wo_done, (half * LAYERS + LAYERS) * H)
                        elif first and u == 1:
                            sp.wait_ge(wk_done, (half * LAYERS + LAYERS) * H + 2)
                        elif not first:
                            sp.wait_ge(w2_ready, half * FB + quad * 4 + (u - 3))
                        sp.dma_start(mlp_stage[u][:, :, :],
                                     mlp_w_d[bass.ds(quad * 4 + u, 1)].rearrange("o p m n -> (o p) m n"))\
                          .then_inc(mstage_ld[u], 16)
                    if first:
                        sp.wait_ge(cr_clear, half + 2)
                        ctx_again(0)
                        sp.wait_ge(n_lo, half * 6 + 6)
                        sp.dma_start(x_next[:, :, :], out_d[1]).then_inc(xn_ld, 16)
                        ctx_again(1)
                    if last:
                        ctx_again(2)
                        ctx_again(3)
                ends_apart(sp, QUADS, load_mlp)

                for m in range(DC):
                    sp.wait_ge(m_add, half * FB * DC + (DC * (FB - 1) + m + 1))
                    sp.dma_start(out_d[bass.ds(half, 1), :, m, :].rearrange("o p n -> (o p) n"), y_out[:, m, :])\
                      .then_inc(landed, 16)
            sp.wait_ge(landed, (HALVES * DC + 1) * 16)

        @block.gpsimd
        def _(pool):
            def copy(out, in_):
                return nc.gpsimd.tensor_tensor(out, in_, zero_col[0:in_.shape[0], :].broadcast_to(tuple(in_.shape)), ALU.add)

            nc.gpsimd.memset(zero_col[:, :], 0.0).then_inc(const0, 1)
            nc.gpsimd.memset(ident[:, :], 0.0).then_inc(const0, 1)
            pool.wait_ge(const0, 2)
            nc.gpsimd.affine_select(out=ident[:, :], in_=ident[:, :], compare_op=ALU.not_equal, fill=1.0, base=0,
                                    pattern=[[-1, P]], channel_multiplier=1).then_inc(const_ready, 1)
            for part in (c_hi, c_lo):
                v = part[:, :, :].rearrange("p c (b t) -> p c b t", t=T)
                nc.gpsimd.memset(v[:, :, :, 0].bitcast(F32), 0.0).then_inc(const_ready, 1)

            def ctx_rows_lo(b, done):
                pool.wait_ge(cr_hi_s, done + 1)
                nc.gpsimd.tensor_tensor(r_lo[0:CH, 3 * b:3 * b + 3, :], cr_stage[0:CH, :, :],
                                        r_hi[0:CH, 3 * b:3 * b + 3, :].bitcast(F32), ALU.subtract).then_inc(cr_lo_s, 1)

            def split_one(hi, lo, slot, u, hi_s, done, pairs_before):
                copy(hi, stage[slot][:, u, :]).then_inc(hi_s, 1)
                pool.wait_ge(hi_s, pairs_before * 2 + (u + 1))
                nc.gpsimd.tensor_tensor(lo, stage[slot][:, u, :], hi.bitcast(F32), ALU.subtract).then_inc(done, 1)

            for turn in range(TURNS):
                for b in range(NB):
                    ctx_rows_lo(b, turn * NB + b)
            pool.wait_ge(stage_ld[1], 16)
            for u in range(2):
                split_one(wq_hi[:, u, :], wq_lo[:, u, :], 1, u, wq_hi_s, wq_done, 0)
            pool.wait_ge(stage_ld[1], 32)
            for u in range(2):
                split_one(wk_hi[:, u, :], wk_lo[:, u, :], 1, u, wk_hi_s, wk_done, 0)

            with pool.Fori(0, HALVES) as half:
                with pool.Fori(0, LAYERS) as l:
                    ph = half * LAYERS + l
                    pool.wait_ge(x_ready, x_is(half, 0) + l)
                    pg = ph * PAIRS

                    def split_wq(pair, first):
                        pool.wait_ge(stage_ld[1], (pg + pair) * 32 + 16)
                        for u in range(2):
                            wait(pool, q_mm, (pg + pair) * 2, u - 1, first)
                            split_one(wq_hi[:, u, :], wq_lo[:, u, :], 1, u, wq_hi_s, wq_done, pg + pair)

                    def split_wk(pair, first):
                        pool.wait_ge(stage_ld[1], (pg + pair) * 32 + 32)
                        for u in range(2):
                            wait(pool, k_mm, (pg + pair) * STEPS, u - 1, first)
                            split_one(wk_hi[:, u, :], wk_lo[:, u, :], 1, u, wk_hi_s, wk_done, pg + pair)

                    def split_wv(pair, first):
                        pool.wait_ge(stage_ld[0], (pg + pair) * 32 + 16)
                        for u in range(2):
                            wait(pool, o_mm, (pg + pair) * 2, u - 1, first)
                            split_one(wv_hi[:, u, :], wv_lo[:, u, :], 0, u, wv_hi_s, wv_done, pg + pair)

                    def split_wo(pair, u, first):
                        if u == 0:
                            pool.wait_ge(stage_ld[0], (pg + pair) * 32 + 32)
                        wait(pool, y_mm, (pg + pair) * 8, 4 * u, first)
                        split_one(wo_hi[:, :], wo_lo[:, :], 0, u, wo_hi_s, wo_done, pg + pair)

                    def split_last_wo():
                        end = pg + PAIRS
                        pool.wait_ge(s_mm, end * STEPS)
                        split_one(last_wo_hi, last_wo_lo, 0, 1, wo_hi_s, wo_done, end - 1)

                    def split_pair(pair, first, last):
                        if not first:
                            split_wo(pair - 1, 0, isinstance(pair, int) and pair == 1)
                        split_wq(pair + 1, False)
                        if not first:
                            split_wo(pair - 1, 1, False)
                        if last:
                            split_wv(pair, first)
                        split_wk(pair + 1, False)
                        if not last:
                            split_wv(pair, first)

                    split_pair(0, True, False)
                    split_pair(1, False, False)
                    with pool.Fori(2, PAIRS - 1) as pair:
                        split_pair(pair, False, False)
                    split_pair(PAIRS - 1, False, True)
                    split_wo(PAIRS - 1, 0, False)
                    split_last_wo()

                pool.wait_ge(x_ready, x_is(half, LAYERS))

                def w1_low(fb, k):
                    pool.wait_ge(w1_hi_s, fb + (k + 1))
                    nc.gpsimd.tensor_tensor(w1_lo[:, k % 2, :], mlp_stage[k % 4][:, 0, :],
                                            w1_hi[:, k % 2, :].bitcast(F32), ALU.subtract).then_inc(w1_ready, 1)

                def w2_low(fb, k):
                    pool.wait_ge(w2_hi_s, fb + (k + 1))
                    nc.gpsimd.tensor_tensor(w2_lo[:, k % 2, :], mlp_stage[k % 4][:, 1, :],
                                            w2_hi[:, k % 2, :].bitcast(F32), ALU.subtract).then_inc(w2_ready, 1)

                def split_mlp(quad, first, last):
                    fb = half * FB + quad * 4
                    for u in range(4):
                        if not (last and u >= 2):
                            w1_low(fb, u + 2)
                        if not (last and u == 3):
                            w2_low(fb, u + 1)
                        if first and u == 1 or last and u == 0:
                            b = 2 if last else 1
                            ctx_rows_lo(b, half * NB + (TURNS * NB + b))
                w1_low(half * FB, 0)
                w2_low(half * FB, 0)
                w1_low(half * FB, 1)
                ctx_rows_lo(0, half * NB + TURNS * NB)
                ends_apart(pool, QUADS, split_mlp)
                ctx_rows_lo(3, half * NB + (TURNS * NB + 3))

        @block.tensor
        def _(pe):
            def mm3(out, w_hi, w_lo, x_hi, x_lo, start=True, stop=True):
                pe.matmul(out, w_hi, x_hi, start=start, stop=False)
                pe.matmul(out, w_hi, x_lo, start=False, stop=False)
                return pe.matmul(out, w_lo, x_hi, start=False, stop=stop)

            def product(out, w_hi, w_lo, x_hi, x_lo):
                for c in range(DC):
                    mm = mm3(out, w_hi(c), w_lo(c), x_hi(c), x_lo(c), start=(c == 0), stop=(c == DC - 1))
                return mm

            def single_head():
                for j in range(2):
                    for c in range(DC):
                        pe.wait_ge(l0w_ld[j * DC + c], 32)
                        for g in range(DC):
                            mm = pe.matmul(bank[j * DC + g], chunk(l0w[2 * j][:, c, :], g), l0w[2 * j + 1][:, c, :],
                                           start=(c == 0), stop=(c == DC - 1))
                            if c == DC - 1:
                                mm.then_inc(lw_mm, 1)

                def scores0(turn, b):
                    pe.wait_ge(ct_lo_s, turn * NB + b + 1)
                    ctx_b = slice(b * T, (b + 1) * T)
                    product(bank[4 + b % 2][0:L, 0:T], lambda c: q2_hi[:, c, batch(b)], lambda c: q2_lo[:, c, batch(b)],
                            lambda c: c_hi[:, c, ctx_b], lambda c: c_lo[:, c, ctx_b]).then_inc(ls_mm, 1)

                def turned(turn, b):
                    done = turn * NB + b
                    pe.wait_ge(lu_copied, done + 1)
                    if b >= 1:
                        pe.wait_ge(lu_lo, done)
                    for m in range(DC):
                        mm = pe.transpose(bank[0][:, m * L:(m + 1) * L], chunk(u_rows[0:L, :], m), ident[0:L, 0:L])
                    mm.then_inc(lt_mm, 1)

                for turn in range(TURNS):
                    xs_hi, xs_lo = ((h_hi, h_lo), (x1_hi, x1_lo))[turn]
                    pe.wait_ge(x_lo_s, turn + 1)
                    if turn == 0:
                        pe.wait_ge(lw_lo, DC)
                    else:
                        pe.wait_ge(y_add, DC)
                    for m in range(DC):
                        product(bank[m][:, 0:N], lambda c: chunk(qk_hi[:, c, :], m), lambda c: chunk(qk_lo[:, c, :], m),
                                lambda c: xs_hi[:, c, :], lambda c: xs_lo[:, c, :]).then_inc(lq_mm, 1)
                    pe.wait_ge(lw_lo, 8)
                    pe.wait_ge(lq_lo, turn * DC + DC)
                    pe.wait_ge(const_ready, 7)
                    scores0(turn, 0)
                    for b in range(NB):
                        done = turn * NB + b
                        pe.wait_ge(ls_norm, done + 1)
                        for t, (t0, rows) in enumerate(CHUNKS):
                            mm = pe.transpose(bank[6][0:rows, t * L:(t + 1) * L], prob0[0:L, t0:t0 + rows],
                                              ident[0:L, 0:L])
                        mm.then_inc(lp_mm, 1)
                        if b + 1 < NB:
                            scores0(turn, b + 1)
                        if b >= 1:
                            turned(turn, b - 1)
                        pe.wait_ge(lp_lo, done + 1)
                        pe.wait_ge(cr_lo_s, done + 1)
                        if done >= 1:
                            pe.wait_ge(lu_copied, done)
                        for t, (_, rows) in enumerate(CHUNKS):
                            mm = mm3(bank[7][0:L, :], p0_hi[0:rows, t, :], p0_lo[0:rows, t, :],
                                     r_hi[0:rows, 3 * b + t, :], r_lo[0:rows, 3 * b + t, :],
                                     start=(t == 0), stop=(t == 2))
                        mm.then_inc(lu_mm, 1)
                    turned(turn, NB - 1)
                    pe.wait_ge(lu_lo, turn * NB + NB)
                    for m in range(DC):
                        product(bank[m][:, 0:N], lambda c: chunk(vo_hi[:, c, :], m), lambda c: chunk(vo_lo[:, c, :], m),
                                lambda c: h_hi[:, c, :], lambda c: h_lo[:, c, :]).then_inc(ld_mm, 1)

            def norm_sums(k2, between=None):
                for n in range(2):
                    for c in range(DC):
                        mm = pe.matmul(bank[5 + n][:, 0:NQ], mean_w[:, :], xT[:, c, piece(n)], start=(c == 0),
                                       stop=(c == DC - 1))
                    mm.then_inc(n_mean, 1)
                if between is not None:
                    between()
                for n in range(2):
                    pe.wait_ge(n_sq, k2 + n + 1)
                    for c in range(DC):
                        mm = pe.matmul(bank[3 + n][:, 0:NQ], mean_w[:, :], sq[:, n, c, :], start=(c == 0),
                                       stop=(c == DC - 1))
                    mm.then_inc(n_var, 1)

            def layer(half, l):
                ph = half * LAYERS + l
                pe.wait_ge(x_ready, x_is(half, 0) + l)

                def keys(pair, i, first):
                    pg = ph * PAIRS + pair
                    b, u = divmod(i, 2)
                    ctx_b = slice(b * T, (b + 1) * T)
                    if b == 0:
                        pe.wait_ge(wk_done, pg * 2 + (u + 1))
                    wait(pe, k_lo_s, pg * STEPS, i, first)
                    product(bank[K_BANK][:, 0:T], lambda c: chunk(wk_hi[:, u, :], c), lambda c: chunk(wk_lo[:, u, :], c),
                            lambda c: c_hi[:, c, ctx_b], lambda c: c_lo[:, c, ctx_b]).then_inc(k_mm, 1)

                pe.wait_ge(ct_lo_s, ctx_parts(half) - 1)
                norm_sums(half * 6 + l * 2, lambda: keys(0, 0, True))
                keys(0, 1, True)
                pe.wait_ge(n_lo, half * 6 + l * 2 + 2)
                pe.wait_ge(ct_lo_s, ctx_parts(half))
                pe.wait_ge(cr_lo_s, ctx_parts(half))

                def queries(pair2, u, r):
                    pe.wait_ge(wq_done, pair2 + (u + 1))
                    product(bank[R_BANK + r][:, 0:N], lambda c: chunk(wq_hi[:, u, :], c), lambda c: chunk(wq_lo[:, u, :], c),
                            lambda c: h_hi[:, c, :], lambda c: h_lo[:, c, :]).then_inc(q_mm, 1)

                def prob_rows(st, i, first):
                    pe.wait_ge(s_norm, st + (i + 1))
                    wait(pe, pt_lo_s, st, i, first)
                    for t, (t0, rows) in enumerate(CHUNKS):
                        mm = pe.transpose(bank[PT_BANK][0:rows, t * L:(t + 1) * L], prob[0:L, t0:t0 + rows],
                                          ident[0:L, 0:L])
                    mm.then_inc(pt_mm, 1)

                def attend(st, b, first, added_before=None):
                    pe.wait_ge(pt_lo_s, st + (2 * b + 2))
                    if added_before is not None:
                        pe.wait_ge(y_add, added_before)
                    for m in range(DC):
                        if m % 2 == 0:
                            wait(pe, u_lo_s, st, 2 * b - 1 + m // 2, first)
                        out = bank[U_BANK + m // 2][:, (m % 2) * 2 * L:(m % 2 + 1) * 2 * L]
                        for t, (_, rows) in enumerate(CHUNKS):
                            mm = mm3(out, chunk(r_hi[0:rows, 3 * b + t, :], m), chunk(r_lo[0:rows, 3 * b + t, :], m),
                                     pT_hi[0:rows, t, :, :], pT_lo[0:rows, t, :, :], start=(t == 0), stop=(t == 2))
                        if m % 2 == 1:
                            mm.then_inc(u_mm, 1)

                def outputs_part(pg, u, b0, b1):
                    columns = slice(b0 * L, b1 * L)
                    out = bank[R_BANK + 1 + u][:, columns]
                    pe.wait_ge(u_lo_s, pg * STEPS - (STEPS - 2 * b1))
                    pe.wait_ge(dv_lo_s, pg)
                    pe.wait_ge(pb_s, pg * NB - (NB - b1))
                    pe.wait_ge(wv_done, pg * 2 - 1 + u)
                    for c in range(DC):
                        mm3(out, chunk(wv_hi[:, u, :], c), chunk(wv_lo[:, u, :], c), u_hi[:, c, u, columns],
                            u_lo[:, c, u, columns], start=(c == 0), stop=False)
                    mm = pe.matmul(out, dv3[:, u * P:(u + 1) * P], pb3[:, u, columns], start=False, stop=True)
                    if b1 == NB:
                        mm.then_inc(o_mm, 1)

                def project(pg, ya, u, st=None, wo=(wo_hi, wo_lo)):
                    pe.wait_ge(o_lo_s, pg * 2 - 1 + u)
                    pe.wait_ge(wo_done, pg * 2 - 1 + u)
                    for m in range(DC):
                        y = u * DC + m
                        if st is not None and y in (2, 3, 7):
                            pe.wait_ge(u_lo_s, st + {2: 1, 3: 2, 7: 3}[y])
                        before = {4: 0, 5: 1, 7: 2}.get(y)
                        if before is not None:
                            pe.wait_ge(y_add, ya + (before + 1))
                        mm3(bank[Y_BANKS[y]][:, 0:N], chunk(wo[0], m), chunk(wo[1], m), o_hi[:, u, :], o_lo[:, u, :])\
                            .then_inc(y_mm, 1)

                def pair_steps(pair, first, last):
                    pg = ph * PAIRS + pair
                    st = pg * STEPS
                    ya = added(half, l) + (pair - 1) * 8
                    for i in range(STEPS):
                        if not (first and i < 2):
                            keys(pair, i, first)
                        if i == 0:
                            if not first:
                                attend((pg - 1) * STEPS, 2, False, ya)
                            queries(pg * 2, 0, 1)
                        if i == 1:
                            queries(pg * 2, 1, 0)
                        if i == 2 and not first:
                            attend((pg - 1) * STEPS, 3, False)
                        if i == 3 and not first:
                            for head in range(2):
                                outputs_part(pg, head, 0, NB)
                        if i == 4 or i == 6:
                            attend(st, i // 2 - 2, first, ya + 4 if i == 6 and not first else None)
                        if i == 5 and not first:
                            project(pg, ya, 0, st)
                        if i == 7 and not first:
                            project(pg, ya, 1, st)
                        if not first or i >= 2:
                            prob_rows(*steps_before(st, i - 2, first))
                        if i >= 1:
                            scores_at(pg, i - 1, first)
                        elif not first:
                            scores_at(pg - 1, STEPS - 1, False)

                def scores_at(pg, i, first):
                    b, u = divmod(i, 2)
                    pe.wait_ge(k_lo_s, pg * STEPS + (i + 1))
                    if b == 0:
                        pe.wait_ge(kcol_lo, pg * 2 + (u + 1))
                        pe.wait_ge(q_lo_s, pg * 2 + (u + 1))
                    wait(pe, s_exp, pg * STEPS, i, first)
                    mm3(bank[S_BANK][0:L, 0:T], q_hi[:, u, batch(b)], q_lo[:, u, batch(b)],
                        k_hi[:, u, :], k_lo[:, u, :]).then_inc(s_mm, 1)

                ends_apart(pe, PAIRS, pair_steps)
                end = ph * PAIRS + (PAIRS - 1)
                ya = added(half, l) + (PAIRS - 1) * 8
                attend(end * STEPS, 2, False, ya)
                prob_rows(end * STEPS, STEPS - 2, False)
                scores_at(end, STEPS - 1, False)
                for u in range(2):
                    outputs_part(end + 1, u, 0, NB - 1)
                prob_rows(end * STEPS, STEPS - 1, False)
                attend(end * STEPS, 3, False)
                for u in range(2):
                    outputs_part(end + 1, u, NB - 1, NB)
                project(end + 1, ya, 0)
                project(end + 1, ya, 1, None, (last_wo_hi, last_wo_lo))

            def mlp_block(half):
                pe.wait_ge(x_ready, x_is(half, LAYERS))
                norm_sums(half * 6 + 4)
                pe.wait_ge(n_lo, half * 6 + 6)

                def hidden(fb, u, first):
                    pe.wait_ge(w1_ready, fb + (u + 1))
                    wait(pe, g_gelu, fb, u - 1, first)
                    product(bank[u % 2][:, 0:N], lambda c: chunk(w1_hi[:, u % 2, :], c),
                            lambda c: chunk(w1_lo[:, u % 2, :], c), lambda c: h_hi[:, c, :], lambda c: h_lo[:, c, :])\
                        .then_inc(g_mm, 1)

                def mlp_steps(quad, first, last):
                    fb = half * FB + quad * 4
                    for u in range(4):
                        if not (last and u == 3):
                            hidden(fb, u + 1, first)
                        pe.wait_ge(w2_ready, fb + (u + 1))
                        pe.wait_ge(g_lo_s, fb + (u + 1))
                        for m in range(DC):
                            wait(pe, m_add, fb * DC, (u - 1) * DC + m + 1, first)
                            mm3(bank[2 + m][:, 0:N], chunk(w2_hi[:, u % 2, :], m), chunk(w2_lo[:, u % 2, :], m),
                                g_hi[:, u % 2, :], g_lo[:, u % 2, :]).then_inc(m_mm, 1)

                hidden(half * FB, 0, True)
                ends_apart(pe, QUADS, mlp_steps)

            single_head()
            with pe.Fori(0, HALVES) as half:
                with pe.Fori(0, LAYERS) as l:
                    layer(half, l)
                mlp_block(half)

        @block.scalar
        def _(act):
            def copy(out, in_):
                return nc.scalar.activation(out, in_, ACT.Copy)

            def split_ctx_hi(b, done):
                act.wait_ge(ct_ld, done * 16 + 16)
                copy(c_hi[:, :, b * T + 1:(b + 1) * T], ct_stage[:, :, :]).then_inc(ct_hi_s, 1)
                act.wait_ge(cr_ld, done * 48 + 48)
                copy(r_hi[0:CH, 3 * b:3 * b + 3, :], cr_stage[0:CH, :, :]).then_inc(cr_hi_s, 1)

            def single_head():
                for j in range(2):
                    for c in range(DC):
                        act.dma_start(l0w[2 * j][:, c, :], l0w_d[2 * j, :, c, :]).then_inc(l0w_ld[j * DC + c], 16)
                        act.dma_start(l0w[2 * j + 1][:, c, :], l0w_d[2 * j + 1, :, c, :]).then_inc(l0w_ld[j * DC + c], 16)

                def weights_hi(j):
                    for g in range(j * DC, j * DC + DC):
                        act.wait_ge(lw_mm, g + 1)
                        copy((qk_hi, vo_hi)[j][:, g % DC, :], bank[g]).then_inc(lw_hi, 1)

                def queries_hi(turn):
                    for m in range(DC):
                        act.wait_ge(lq_mm, turn * DC + m + 1)
                        copy(q2_hi[:, m, :], bank[m][:, 0:N]).then_inc(lq_hi, 1)

                def exp0(turn, b):
                    act.wait_ge(ls_neg, turn * NB + b + 1)
                    st = stats[0:L, b % 2, :]
                    nc.scalar.activation(prob0[0:L, 1:T], bank[4 + b % 2][0:L, 1:T], ACT.Exp, bias=st[:, 1:2],
                                         scale=FULL_SCALE, accum_out=st[:, 2:3]).then_inc(ls_exp, 1)

                def turned_hi(turn, b):
                    act.wait_ge(lt_mm, turn * NB + b + 1)
                    copy(h_hi[:, :, batch(b)], bank[0][:, 0:DC * L].rearrange("p (m q) -> p m q", q=L)).then_inc(lu_hi, 1)

                def batches(turn, between):
                    exp0(turn, 0)
                    for b in range(NB):
                        act.wait_ge(lp_mm, turn * NB + b + 1)
                        copy(p0_hi[0:CH, :, :].rearrange("p t q -> p (t q)"), bank[6][0:CH, 0:3 * L]).then_inc(lp_hi, 1)
                        if b + 1 < NB:
                            exp0(turn, b + 1)
                        if b >= 1:
                            turned_hi(turn, b - 1)
                        act.wait_ge(lu_mm, turn * NB + b + 1)
                        copy(u_rows[0:L, :], bank[7][0:L, :]).then_inc(lu_copied, 1)
                        between(b)
                    turned_hi(turn, NB - 1)

                act.wait_ge(x_ld[0], 16)
                copy(h_hi[:, :, :], xT[:, :, :]).then_inc(x_hi_s, 1)
                split_ctx_hi(0, 0)
                split_ctx_hi(1, 1)
                weights_hi(0)
                split_ctx_hi(2, 2)
                weights_hi(1)
                queries_hi(0)


                def beside_first(b):
                    if b == 0:
                        split_ctx_hi(3, 3)
                    if b == 2:
                        split_ctx_hi(0, 4)
                batches(0, beside_first)
                act.wait_ge(x_ld[1], 16)
                copy(x1_hi[:, :, :], x1[:, :, :]).then_inc(x_hi_s, 1)
                split_ctx_hi(1, 5)
                split_ctx_hi(2, 6)
                queries_hi(1)
                batches(1, lambda b: split_ctx_hi(3, 7) if b == 0 else None)

            def load_table(function):
                nc.scalar.activation(unused[:, :], eps_col[:, :], function)

            def norm_act(k2, after_squares, after_roots, next_function):
                load_table(ACT.Sqrt)
                for n in range(2):
                    act.wait_ge(n_cen, k2 + n + 1)
                    nc.scalar.activation(sq[:, n, :, :], cen[:, n, :, :], ACT.Square).then_inc(n_sq, 1)
                after_squares()
                for n in range(2):
                    act.wait_ge(n_var, k2 + n + 1)
                    nc.scalar.activation(rstd[:, n, :], bank[3 + n][:, 0:NQ], ACT.Sqrt, bias=eps_col[:, :])\
                      .then_inc(n_sd, 1)
                load_table(next_function)
                after_roots()
                for n in range(2):
                    act.wait_ge(n_scaled, k2 + n + 1)
                    for c in range(DC):
                        h = nc.scalar.activation(h_hi[:, c, piece(n)], cen[:, n, c, :], ACT.Identity,
                                                 bias=norm_p[:, c, OFFSET_COL:OFFSET_COL + 1])
                    h.then_inc(n_hi, 1)

            def layer(half, l):
                ph = half * LAYERS + l

                def keys_hi(pair, i, first):
                    pg = ph * PAIRS + pair
                    st = pg * STEPS
                    u = i % 2
                    act.wait_ge(k_mm, st + (i + 1))
                    if i == 0:
                        act.wait_ge(bk_ready, pg + 1)
                    wait(act, s_mm, st, i - 1, first)
                    nc.scalar.activation(k_hi[:, u, 1:T], bank[K_BANK][:, 1:T], ACT.Identity,
                                         bias=bk_c[:, u:u + 1]).then_inc(k_hi_s, 1)

                norm_act(half * 6 + l * 2, lambda: keys_hi(0, 0, True), lambda: None, ACT.Exp)
                act.wait_ge(n_lo, half * 6 + l * 2 + 2)
                act.wait_ge(landed, half * (DC * 16) + 16)

                def exps(st, i, first):
                    act.wait_ge(s_neg, st + (i + 1))
                    wait(act, pt_mm, st, i, first)
                    stat = stats[0:L, i % 2, :]
                    nc.scalar.activation(prob[0:L, :], bank[S_BANK][0:L, 0:T], ACT.Exp, bias=stat[:, 1:2],
                                         scale=HEAD_SCALE, accum_out=stat[:, 2:3]).then_inc(s_exp, 1)

                def prob_hi(pg, i, first):
                    b, u = divmod(i, 2)
                    act.wait_ge(pt_mm, pg * STEPS + (i + 1))
                    if u == 0:
                        wait(act, pb_s, pg * NB, b, first)
                    copy(pT_hi[0:CH, :, u, :], bank[PT_BANK][0:CH, 0:3 * L].rearrange("p (t q) -> p t q", q=L))\
                        .then_inc(pt_hi_s, 1)

                def attended_hi(st, b):
                    for a in range(2):
                        act.wait_ge(u_mm, st + (2 * b + a + 1))
                        copy(u_hi[:, 2 * a:2 * a + 2, :, batch(b)],
                             bank[U_BANK + a][:, 0:4 * L].rearrange("p (m u q) -> p m u q", u=2, q=L)).then_inc(u_hi_s, 1)

                def outputs_hi(pg, u):
                    act.wait_ge(o_mm, pg * 2 - 1 + u)
                    if u == 0:
                        act.wait_ge(bv_ready, pg)
                    nc.scalar.activation(o_hi[:, u, :], bank[R_BANK + 1 + u][:, 0:N], ACT.Identity,
                                         bias=bv_c[:, u:u + 1]).then_inc(o_hi_s, 1)

                def q_hi_of(pg, u, r):
                    act.wait_ge(q_mm, pg * 2 + (u + 1))
                    if u == 0:
                        act.wait_ge(bq_ready, pg + 1)
                    nc.scalar.activation(q_hi[:, u, :], bank[R_BANK + r][:, 0:N], ACT.Identity,
                                         bias=bq_c[:, u:u + 1]).then_inc(q_hi_s, 1)

                def pair_steps(pair, first, last):
                    pg = ph * PAIRS + pair
                    st = pg * STEPS
                    for i in range(STEPS):
                        u = i % 2
                        if not (first and i == 0):
                            keys_hi(pair, i, first)
                        if i == 0:
                            if not first:
                                attended_hi((pg - 1) * STEPS, 2)
                            q_hi_of(pg, 0, 1)
                        if i == 1:
                            q_hi_of(pg, 1, 0)
                        if i == 2 and not first:
                            attended_hi((pg - 1) * STEPS, 3)
                        if i == 3 and not first:
                            outputs_hi(pg, 0)
                        if i == 4 or i == 6:
                            attended_hi(st, i // 2 - 2)
                        if i == 5 and not first:
                            outputs_hi(pg, 1)
                        if i >= 2:
                            prob_hi(pg, i - 2, first)
                        elif not first:
                            prob_hi(pg - 1, STEPS + i - 2, False)
                        if not first or i >= 1:
                            exps(*steps_before(st, i - 1, first))

                ends_apart(act, PAIRS, pair_steps)
                end = ph * PAIRS + (PAIRS - 1)
                attended_hi(end * STEPS, 2)
                prob_hi(end, STEPS - 2, False)
                exps(end * STEPS, STEPS - 1, False)
                prob_hi(end, STEPS - 1, False)
                attended_hi(end * STEPS, 3)
                outputs_hi(end + 1, 0)
                outputs_hi(end + 1, 1)

            def mlp_block(half):
                def w1_high(quad, k, first):
                    act.wait_ge(mstage_ld[k % 4], half * (QUADS * 16) + (quad + k // 4) * 16 + 16)
                    wait(act, g_mm, half * FB + quad * 4, k - 1, first)
                    copy(w1_hi[:, k % 2, :], mlp_stage[k % 4][:, 0, :]).then_inc(w1_hi_s, 1)

                def w2_high(quad, k, first):
                    act.wait_ge(mstage_ld[k % 4], half * (QUADS * 16) + (quad + k // 4) * 16 + 16)
                    wait(act, m_mm, (half * FB + quad * 4) * DC, (k - 1) * DC, first)
                    copy(w2_hi[:, k % 2, :], mlp_stage[k % 4][:, 1, :]).then_inc(w2_hi_s, 1)

                norm_act(half * 6 + 4, lambda: None, lambda: w1_high(0, 0, True), ACT.Gelu)
                w2_high(0, 0, True)
                w1_high(0, 1, True)
                act.wait_ge(n_lo, half * 6 + 6)

                def mlp_act(quad, first, last):
                    fb = half * FB + quad * 4
                    for u in range(4):
                        act.wait_ge(g_mm, fb + (u + 1))
                        act.wait_ge(mlp_b_ready, fb + (u + 1))
                        wait(act, g_lo_s, fb, u - 1, first)
                        nc.scalar.activation(gelu[:, u % 2, :], bank[u % 2][:, 0:N], ACT.Gelu,
                                             bias=mlp_b_c[:, u % 2:u % 2 + 1])\
                          .then_inc(g_gelu, 1)
                        act.wait_ge(g_gelu, fb + (u + 1))
                        wait(act, m_mm, fb * DC, DC * (u - 1), first)
                        copy(g_hi[:, u % 2, :], gelu[:, u % 2, :]).then_inc(g_hi_s, 1)
                        if not (last and u >= 2):
                            w1_high(quad, u + 2, first)
                        if not (last and u == 3):
                            w2_high(quad, u + 1, first)
                        if first and u == 1 or last and u == 0:
                            b = 2 if last else 1
                            split_ctx_hi(b, half * NB + (TURNS * NB + b))
                split_ctx_hi(0, half * NB + TURNS * NB)
                ends_apart(act, QUADS, mlp_act)
                split_ctx_hi(3, half * NB + (TURNS * NB + 3))

            single_head()
            act.wait_ge(const_ready, 7)
            with act.Fori(0, HALVES) as half:
                with act.Fori(0, LAYERS) as l:
                    layer(half, l)
                mlp_block(half)

        @block.vector
        def _(dve):
            sub = ALU.subtract

            def low(out, value, hi):
                return nc.vector.tensor_tensor(out, value, hi.bitcast(F32), sub)

            def low_biased(out, value, bias, hi):
                return nc.vector.scalar_tensor_tensor(out=out, in0=value, scalar=bias, in1=hi.bitcast(F32), op0=ALU.add,
                                                      op1=sub)

            def block_done():
                nc.vector.memset(flag[:, :], 0.0).then_inc(x_ready, 1)

            def maxima(st, scores, scale, mm, max_s, neg_s, count):
                dve.wait_ge(mm, count)
                nc.vector.reduce_max(st[:, 0:1], scores, AX_X).then_inc(max_s, 1)
                dve.wait_ge(max_s, count)
                nc.vector.tensor_scalar(st[:, 1:2], st[:, 0:1], -scale, None, ALU.mult).then_inc(neg_s, 1)

            def normalise(st, p, exp_s, rcp_s, norm_s, count):
                dve.wait_ge(exp_s, count)
                nc.vector.reciprocal(st[:, 3:4], st[:, 2:3]).then_inc(rcp_s, 1)
                dve.wait_ge(rcp_s, count)
                nc.vector.tensor_scalar(p, p, st[:, 3:4], None, ALU.mult).then_inc(norm_s, 1)

            def split_ctx_lo(b, done):
                dve.wait_ge(ct_hi_s, done + 1)
                ctx_b = slice(b * T + 1, (b + 1) * T)
                low(c_lo[:, :, ctx_b], ct_stage[:, :, :], c_hi[:, :, ctx_b]).then_inc(ct_lo_s, 1)

            def single_head():
                nc.vector.memset(cr_stage[:, :, :], 0.0).then_inc(cr_clear, 1)

                def weights_lo(j):
                    for g in range(j * DC, j * DC + DC):
                        dve.wait_ge(lw_hi, g + 1)
                        low((qk_lo, vo_lo)[j][:, g % DC, :], bank[g], (qk_hi, vo_hi)[j][:, g % DC, :]).then_inc(lw_lo, 1)

                def queries_lo(turn):
                    for m in range(DC):
                        dve.wait_ge(lq_hi, turn * DC + m + 1)
                        low(q2_lo[:, m, :], bank[m][:, 0:N], q2_hi[:, m, :]).then_inc(lq_lo, 1)

                def softmax0(turn, b):
                    st = stats[0:L, b % 2, :]
                    count = turn * NB + b + 1
                    maxima(st, bank[4 + b % 2][0:L, 1:T], FULL_SCALE, ls_mm, ls_max, ls_neg, count)
                    normalise(st, prob0[0:L, 1:T], ls_exp, ls_rcp, ls_norm, count)

                def turned_lo(turn, b):
                    dve.wait_ge(lu_hi, turn * NB + b + 1)
                    low(h_lo[:, :, batch(b)], bank[0][:, 0:DC * L].rearrange("p (m q) -> p m q", q=L),
                        h_hi[:, :, batch(b)]).then_inc(lu_lo, 1)

                def batches(turn, between):
                    softmax0(turn, 0)
                    for b in range(NB):
                        dve.wait_ge(lp_hi, turn * NB + b + 1)
                        low(p0_lo[0:CH, :, :].rearrange("p t q -> p (t q)"), bank[6][0:CH, 0:3 * L],
                            p0_hi[0:CH, :, :].rearrange("p t q -> p (t q)")).then_inc(lp_lo, 1)
                        if b + 1 < NB:
                            softmax0(turn, b + 1)
                        if b >= 1:
                            turned_lo(turn, b - 1)
                        between(b)
                    turned_lo(turn, NB - 1)

                def residual(turn, x):
                    for m in range(DC):
                        dve.wait_ge(ld_mm, turn * DC + m + 1)
                        nc.vector.scalar_tensor_tensor(out=xT[:, m, :], in0=bank[m][:, 0:N], scalar=alpha_col[:, 0:1],
                                                       in1=x[:, m, :], op0=ALU.mult, op1=ALU.add).then_inc(y_add, 1)

                dve.wait_ge(x_hi_s, 1)
                low(h_lo[:, :, :], xT[:, :, :], h_hi[:, :, :]).then_inc(x_lo_s, 1)
                split_ctx_lo(0, 0)
                split_ctx_lo(1, 1)
                weights_lo(0)
                split_ctx_lo(2, 2)
                weights_lo(1)
                nc.vector.memset(prob0[:, 0:1], 0.0)
                queries_lo(0)


                def beside_first(b):
                    if b == 0:
                        split_ctx_lo(3, 3)
                    if b == 2:
                        split_ctx_lo(0, 4)
                batches(0, beside_first)
                dve.wait_ge(x_hi_s, 2)
                low(x1_lo[:, :, :], x1[:, :, :], x1_hi[:, :, :]).then_inc(x_lo_s, 1)
                split_ctx_lo(1, 5)
                dve.wait_ge(alpha_ld, 16)
                residual(0, xT)
                split_ctx_lo(2, 6)
                queries_lo(1)
                batches(1, lambda b: split_ctx_lo(3, 7) if b == 0 else None)
                dve.wait_ge(landed, 16)
                residual(1, x1)
                dve.wait_ge(y_add, TURNS * DC)
                block_done()

            def norm_dve(k2, norms, between):
                for n in range(2):
                    dve.wait_ge(n_mean, k2 + n + 1)
                    mean = bank[5 + n][:, 0:NQ].unsqueeze(1).broadcast_to((P, DC, NQ))
                    nc.vector.tensor_tensor(cen[:, n, :, :], xT[:, :, piece(n)], mean, sub).then_inc(n_cen, 1)
                dve.wait_ge(norm_ld, norms * 16 + 16)
                for n in range(2):
                    dve.wait_ge(n_sq, k2 + n + 1)
                    for c in range(DC):
                        f = nc.vector.tensor_scalar(cen[:, n, c, :], cen[:, n, c, :],
                                                    norm_p[:, c, SCALE_COL:SCALE_COL + 1], None, ALU.mult)
                    f.then_inc(n_by_scale, 1)
                between()
                for n in range(2):
                    dve.wait_ge(n_sd, k2 + n + 1)
                    nc.vector.reciprocal(rstd[:, n, :], rstd[:, n, :]).then_inc(n_rstd, 1)
                    dve.wait_ge(n_by_scale, k2 + n + 1)
                    dve.wait_ge(n_rstd, k2 + n + 1)
                    r = rstd[:, n, :].unsqueeze(1).broadcast_to((P, DC, NQ))
                    nc.vector.tensor_tensor(cen[:, n, :, :], cen[:, n, :, :], r, ALU.mult).then_inc(n_scaled, 1)
                for n in range(2):
                    dve.wait_ge(n_hi, k2 + n + 1)
                    for c in range(DC):
                        f = low_biased(h_lo[:, c, piece(n)], cen[:, n, c, :], norm_p[:, c, OFFSET_COL:OFFSET_COL + 1],
                                       h_hi[:, c, piece(n)])
                    f.then_inc(n_lo, 1)
                for c in range(DC):
                    r = nc.vector.tensor_scalar(xT[:, c, :], xT[:, c, :], norm_p[:, c, RES_COL:RES_COL + 1], None,
                                                ALU.add)
                r.then_inc(n_res, 1)

            def layer(half, l):
                ph = half * LAYERS + l
                def column(out, kind, pair, ready, n=2, u=0):
                    src = cols[:, kind, bass.ds(l * H + (pair * 2 + u), n)]
                    return nc.vector.tensor_scalar(out, src, 0.0, None, ALU.add).then_inc(ready, 1)

                def keys_lo(pair, i):
                    pg = ph * PAIRS + pair
                    u = i % 2
                    dve.wait_ge(k_hi_s, pg * STEPS + (i + 1))
                    low_biased(k_lo[:, u, 1:T], bank[K_BANK][:, 1:T], bk_c[:, u:u + 1], k_hi[:, u, 1:T])\
                        .then_inc(k_lo_s, 1)
                    if i < 2:
                        column(k_hi[:, u, 0:1], BIAS_K, pair, kcol_hi, 1, u)
                        dve.wait_ge(kcol_hi, pg * 2 + (u + 1))
                        low(k_lo[:, u, 0:1], cols[:, BIAS_K, bass.ds(l * H + (pair * 2 + u), 1)], k_hi[:, u, 0:1])\
                            .then_inc(kcol_lo, 1)

                def queries_lo(pg, u, r):
                    dve.wait_ge(q_hi_s, pg * 2 + (u + 1))
                    low_biased(q_lo[:, u, :], bank[R_BANK + r][:, 0:N], bq_c[:, u:u + 1], q_hi[:, u, :]).then_inc(q_lo_s, 1)

                def bias_rows(pairs_done):
                    dve.wait_ge(vb_ld, pairs_done * 16)
                    nc.vector.tensor_tensor(dv[:, :], vb_rows[:, 1, :], vb_rows[:, 0, :], sub).then_inc(dv_s, 1)
                    dve.wait_ge(dv_s, pairs_done)
                    nc.vector.tensor_copy(dv3[0:1, :], dv[:, :])
                    nc.vector.tensor_copy(dv3[32:33, :], dv[:, :]).then_inc(dv_hi_s, 1)
                    dve.wait_ge(dv_hi_s, pairs_done)
                    low(dv3[64:65, :], dv[:, :], dv3[0:1, :]).then_inc(dv_lo_s, 1)

                def softmax(st, i):
                    maxima(stats[0:L, i % 2, :], bank[S_BANK][0:L, 0:T], HEAD_SCALE, s_mm, s_max, s_neg, st + (i + 1))
                    normalise(stats[0:L, i % 2, :], prob[0:L, :], s_exp, s_rcp, s_norm, st + (i + 1))

                def prob_lo(pg, i):
                    b, u = divmod(i, 2)
                    dve.wait_ge(pt_hi_s, pg * STEPS + (i + 1))
                    low(pT_lo[0:CH, :, u, :], bank[PT_BANK][0:CH, 0:3 * L].rearrange("p (t q) -> p t q", q=L),
                        pT_hi[0:CH, :, u, :]).then_inc(pt_lo_s, 1)
                    if u == 1:
                        dve.wait_ge(pt_lo_s, pg * STEPS + (i + 1))
                        for row, part in ((0, pT_hi), (32, pT_lo), (64, pT_hi)):
                            kept = nc.vector.tensor_copy(pb3[row:row + 1, :, batch(b)], part[0:1, 0, :, :].bitcast(F32))
                        kept.then_inc(pb_s, 1)

                def attended_lo(st, b):
                    for a in range(2):
                        dve.wait_ge(u_hi_s, st + (2 * b + a + 1))
                        low(u_lo[:, 2 * a:2 * a + 2, :, batch(b)],
                            bank[U_BANK + a][:, 0:4 * L].rearrange("p (m u q) -> p m u q", u=2, q=L),
                            u_hi[:, 2 * a:2 * a + 2, :, batch(b)]).then_inc(u_lo_s, 1)

                def outputs_lo(pg, u):
                    dve.wait_ge(o_hi_s, pg * 2 - 1 + u)
                    low_biased(o_lo[:, u, :], bank[R_BANK + 1 + u][:, 0:N], bv_c[:, u:u + 1], o_hi[:, u, :]).then_inc(o_lo_s, 1)

                def add_pieces(pg, u, ya=None):
                    for m in range(DC):
                        y = u * DC + m
                        if ya is not None:
                            dve.wait_ge(y_add, ya + (m + 1))
                        dve.wait_ge(y_mm, pg * 8 + (y - 7))
                        nc.vector.tensor_tensor(xT[:, m, :], bank[Y_BANKS[y]][:, 0:N], xT[:, m, :], ALU.add)\
                          .then_inc(y_add, 1)

                def pair_steps(pair, first, last):
                    pg = ph * PAIRS + pair
                    st = pg * STEPS
                    for i in range(STEPS):
                        u = i % 2
                        if not (first and i == 0):
                            keys_lo(pair, i)
                        if i == 7 and not last:
                            dve.wait_ge(k_lo_s, st + STEPS)
                            column(bk_c[:, :], BK, pair + 1, bk_ready)
                        if i == 0:
                            if not first:
                                attended_lo((pg - 1) * STEPS, 2)
                            dve.wait_ge(bq_ready, pg + 1)
                            queries_lo(pg, 0, 1)
                        if i == 1:
                            queries_lo(pg, 1, 0)
                        if i == 2:
                            if not last:
                                dve.wait_ge(q_lo_s, pg * 2 + 2)
                                column(bq_c[:, :], BQ, pair + 1, bq_ready)
                            if not first:
                                column(bv_c[:, :], BV, pair - 1, bv_ready)
                                bias_rows(pg)
                                attended_lo((pg - 1) * STEPS, 3)
                        if i == 3 and not first:
                            dve.wait_ge(bv_ready, pg)
                            outputs_lo(pg, 0)
                        if i == 4 or i == 6:
                            attended_lo(st, i // 2 - 2)
                        if i == 5 and not first:
                            add_pieces(pg, 0)
                            outputs_lo(pg, 1)
                        if i == 7 and not first:
                            add_pieces(pg, 1)
                        if i >= 2:
                            prob_lo(pg, i - 2)
                        elif not first:
                            prob_lo(pg - 1, STEPS + i - 2)
                        if i >= 1:
                            softmax(st, i - 1)
                        elif not first:
                            softmax((pg - 1) * STEPS, STEPS - 1)
                        if i == 7 and last:
                            column(bv_c[:, :], BV, pair, bv_ready)
                            bias_rows(pg + 1)

                def first_keys():
                    dve.wait_ge(bk_ready, ph * PAIRS + 1)
                    keys_lo(0, 0)

                column(bq_c[:, :], BQ, 0, bq_ready)
                column(bk_c[:, :], BK, 0, bk_ready)
                norm_dve(half * 6 + l * 2, half * 3 + l, first_keys)
                dve.wait_ge(landed, half * (DC * 16) + 16)
                ends_apart(dve, PAIRS, pair_steps)
                end = ph * PAIRS + (PAIRS - 1)
                attended_lo(end * STEPS, 2)
                prob_lo(end, STEPS - 2)
                softmax(end * STEPS, STEPS - 1)
                prob_lo(end, STEPS - 1)
                attended_lo(end * STEPS, 3)
                dve.wait_ge(bv_ready, end + 1)
                outputs_lo(end + 1, 0)
                outputs_lo(end + 1, 1)
                add_pieces(end + 1, 0)
                add_pieces(end + 1, 1, added(half, l) + (PAIRS - 1) * 8)
                dve.wait_ge(y_add, added(half, l) + PAIRS * 8)
                block_done()

            def mlp_block(half):
                nc.vector.memset(cr_stage[:, :, :], 0.0).then_inc(cr_clear, 1)
                norm_dve(half * 6 + 4, half * 3 + 2, lambda: None)

                def bias(f, u):
                    nc.vector.tensor_scalar(mlp_b_c[:, u % 2:u % 2 + 1], mlp_b[:, bass.ds(f, 1)], 0.0, None, ALU.add)\
                      .then_inc(mlp_b_ready, 1)

                def gate_lo(fb, u):
                    dve.wait_ge(g_hi_s, fb + (u + 1))
                    low(g_lo[:, u % 2, :], gelu[:, u % 2, :], g_hi[:, u % 2, :]).then_inc(g_lo_s, 1)

                def mlp_dve(quad, first, last):
                    fb = half * FB + quad * 4
                    for u in range(4):
                        if not (last and u >= 2):
                            bias(quad * 4 + (u + 2), u)
                        if not (last and u == 3):
                            gate_lo(fb, u + 1)
                        if last and u == 3:
                            split_ctx_lo(3, half * NB + (TURNS * NB + 3))
                            dve.wait_ge(xn_ld, half * 16 + 16)
                        for m in range(DC):
                            dve.wait_ge(m_mm, fb * DC + (u * DC + m + 1))
                            nc.vector.tensor_tensor((y_out if last and u == 3 else xT)[:, m, :], bank[2 + m][:, 0:N],
                                                    xT[:, m, :], ALU.add).then_inc(m_add, 1)
                        if first and u == 1 or last and u == 0:
                            b = 2 if last else 1
                            split_ctx_lo(b, half * NB + (TURNS * NB + b))

                bias(0, 0)
                bias(1, 1)
                split_ctx_lo(0, half * NB + TURNS * NB)
                gate_lo(half * FB, 0)
                ends_apart(dve, QUADS, mlp_dve)
                dve.wait_ge(m_add, half * (FB * DC) + FB * DC)
                nc.vector.tensor_copy(xT[:, :, :], x_next[:, :, :]).then_inc(x_ready, 1)

            nc.vector.memset(mean_w[:, :], 1.0 / D).then_inc(const_ready, 1)
            nc.vector.memset(dv3[:, :].bitcast(F32), 0.0).then_inc(const_ready, 1)
            nc.vector.memset(pb3[:, :, :].bitcast(F32), 0.0).then_inc(const_ready, 1)
            nc.vector.memset(eps_col[:, :], EPS).then_inc(const_ready, 1)
            single_head()
            dve.wait_ge(cols_ld, 16)
            dve.wait_ge(mlp_b_ld, 16)
            with dve.Fori(0, HALVES) as half:
                with dve.Fori(0, LAYERS) as l:
                    layer(half, l)
                mlp_block(half)


def kernel(**inputs):
    import concourse.bacc as _bacc
    from concourse import mybir as _mybir
    from concourse.bass_utils import run_bass_kernel_spmd as _run

    a = {k: np.asarray(v) for k, v in inputs.items()}

    def rows(m):
        return np.moveaxis(m.reshape(m.shape[:-2] + (m.shape[-2] // P, P, m.shape[-1])), -3, -2)

    def head_cols(m):
        return rows(np.moveaxis(m.reshape(D, H, P), 1, 0)).reshape(H, P, D)

    def both(name):
        return np.stack([a[f"L1_xattn_{name}1"], a[f"L1_xattn_{name}2"]])

    def layer_w(i):
        w = {n: a[f"L1_xattn_{n}{i}"] for n in ("wq", "wk", "wv", "wo")}
        m = np.stack([head_cols(w["wq"]), head_cols(w["wk"]), head_cols(w["wv"]), w["wo"].reshape(H, P, D)])
        return m.reshape(4, PAIRS, 2, P, D).transpose(1, 0, 3, 2, 4)

    def norm_cols(*names):
        return np.stack([a[f"L1_xattn_{n}"].reshape(DC, P).T for n in names], 2)

    x = a["x"].reshape(HALVES, N, D)[::-1]
    context = np.concatenate([a["ctx_2048"][NB:], a["ctx_2048"][:NB]])
    pair_w = np.concatenate([layer_w(1), layer_w(2)])
    arrays = {
        "xT": rows(x.transpose(0, 2, 1)),
        "ctxT": rows(np.moveaxis(context, 1, 2)),
        "ctx": context,
        "l0_w": np.stack([rows(a["L0_xattn_w_q"]), rows(a["L0_xattn_w_k"]), rows(a["L0_xattn_w_v"]),
                          rows(a["L0_xattn_w_o"].T)]),
        "alpha": a["L0_xattn_alpha"].reshape(1),
        "pair_w": np.concatenate([pair_w, pair_w[:1]]).reshape((LAYERS * PAIRS + 1) * 4, P, 2, D),
        "cols": np.stack([both(n).reshape(LAYERS * H, P).T for n in ("bq", "bk", "bv", "bias_k")], 1),
        "v_rows": np.stack([both("bv").reshape(LAYERS * PAIRS, 2 * P), both("bias_v").reshape(LAYERS * PAIRS, 2 * P)], 1),
        "norm_p": np.stack([norm_cols("ln1_scale", "ln1_offset", "bo1"), norm_cols("ln2_scale", "ln2_offset", "bo2"),
                            norm_cols("ln_mlp_scale", "ln_mlp_offset", "b_fc2")]),
        "mlp_w": np.stack([head_cols(a["L1_xattn_w_fc1"]), a["L1_xattn_w_fc2"].reshape(FB, P, D)], 2),
        "mlp_b": a["L1_xattn_b_fc1"].reshape(FB, P).T,
    }
    nc = _bacc.Bacc("TRN2", target_bir_lowering=False, num_devices=1)
    feed, args = {}, []
    for name, arr in arrays.items():
        feed[f"{name}_dram"] = np.ascontiguousarray(arr)
        args.append(nc.dram_tensor(f"{name}_dram", arr.shape, _mybir.dt.from_np(arr.dtype), kind="ExternalInput").ap())
    out = nc.dram_tensor("out_dram", (HALVES, P, DC, N), F32, kind="ExternalOutput").ap()
    build(nc, *args, out)
    r = _run(nc, [feed], core_ids=[0])
    return np.ascontiguousarray(r.results[0]["out_dram"].transpose(0, 3, 2, 1)).reshape(B, L, D)
```
